# Optimizing a Trainium2 kernel written in Bass

```python
import numpy as np
import jax
import jax.numpy as jnp

def _softmax(x, axis=-1):
    return jax.nn.softmax(x, axis=axis)

def _gelu(x):
    return jax.nn.gelu(x, approximate=True)

def _silu(x):
    return jax.nn.silu(x)

def _sigmoid(x):
    return jax.nn.sigmoid(x)

def _layernorm(x, axis=-1, eps=1e-05):
    m = jnp.mean(x, axis=axis, keepdims=True)
    v = jnp.var(x, axis=axis, keepdims=True)
    return (x - m) / jnp.sqrt(v + eps)

def _scatter_add(tgt, idx, src, axis=0):
    return tgt.at[idx].add(src)

def _segment_sum(src, seg, n):
    return jax.ops.segment_sum(src, seg, n)
kernel_name = 'mk_xattn_ffn_d4_seqx_r8_46c2b9'

def setup_inputs(seed: int=0):
    np.random.seed(seed)
    _w = jnp.asarray

    def _rec_inputs():
        import jax
        import jax.numpy as jnp
        _rk = jax.random.key(seed)
        x = -0.0002928 + 1 * jax.random.normal(jax.random.fold_in(_rk, 1), (32, 128, 128), jnp.float32)
        _lenS = 128 - jax.random.randint(jax.random.fold_in(_rk, 7), (32,), 0, max(1, 128 // 4) + 1, jnp.int32)
        _lenS2 = 77 - jax.random.randint(jax.random.fold_in(_rk, 8), (32,), 0, max(1, 77 // 4) + 1, jnp.int32)
        _ctx_1024P = jax.random.normal(jax.random.fold_in(_rk, 11), (32, 16, 128), jnp.float32)
        _ctx_1024c = jax.random.dirichlet(jax.random.fold_in(_rk, 511), 0.3 * jnp.ones((16,), jnp.float32), (32, 77))
        _ctx_1024t = jnp.einsum('bsk,bkd->bsd', _ctx_1024c, _ctx_1024P)
        _ctx_1024t = _ctx_1024t * jax.lax.rsqrt(jnp.mean(jnp.square(_ctx_1024t)) + 1e-12) * 0.953939
        ctx_1024 = -1.39393e-06 + 0.999914 * (_ctx_1024t + 0.3 * jax.random.normal(jax.random.fold_in(_rk, 611), (32, 77, 128), jnp.float32))
        return (x, ctx_1024)
    x, ctx_1024 = _rec_inputs()

    def _L0_xattn_setup():
        import jax, jax.numpy as jnp
        import numpy as np
        import math
        D_MODEL = 128
        N_HEADS = 16
        D_HEAD = D_MODEL // N_HEADS
        key = jax.random.key(seed)
        ks = jax.random.split(key, 11)
        N, L, S = (2, 256, 256)
        inp = {'queries': jax.random.normal(ks[0], (N, L, D_MODEL), dtype=jnp.float32), 'keys': jax.random.normal(ks[1], (N, S, D_MODEL), dtype=jnp.float32), 'values': jax.random.normal(ks[2], (N, S, D_MODEL), dtype=jnp.float32), 'Wq': jax.random.normal(ks[3], (D_MODEL, N_HEADS * D_HEAD), dtype=jnp.float32) / math.sqrt(D_MODEL), 'bq': jnp.zeros((N_HEADS * D_HEAD,), dtype=jnp.float32), 'Wk': jax.random.normal(ks[4], (D_MODEL, N_HEADS * D_HEAD), dtype=jnp.float32) / math.sqrt(D_MODEL), 'bk': jnp.zeros((N_HEADS * D_HEAD,), dtype=jnp.float32), 'Wv': jax.random.normal(ks[5], (D_MODEL, N_HEADS * D_HEAD), dtype=jnp.float32) / math.sqrt(D_MODEL), 'bv': jnp.zeros((N_HEADS * D_HEAD,), dtype=jnp.float32), 'Wo': jax.random.normal(ks[6], (N_HEADS * D_HEAD, D_MODEL), dtype=jnp.float32) / math.sqrt(N_HEADS * D_HEAD), 'bo': jnp.zeros((D_MODEL,), dtype=jnp.float32)}
        return inp
    _L0_xattn_all = _L0_xattn_setup()
    _L0_xattn_in = {k: v for k, v in _L0_xattn_all.items() if k in ('Wq', 'bq', 'Wk', 'bk', 'Wv', 'bv', 'Wo', 'bo')}
    del _L0_xattn_all

    def _L0_ffn_setup():
        import jax, jax.numpy as jnp
        import numpy as np
        B, T, D = (4, 256, 128)
        H, DH, E, SEL = (8, 64, 5, 2)

        def _topk_mask(logits, k):
            _, idx = jax.lax.top_k(logits, k)
            return jnp.sum(jax.nn.one_hot(idx, logits.shape[-1], dtype=logits.dtype), axis=-2)
        key = jax.random.key(seed)
        ks = jax.random.split(key, 7)
        s = 0.02
        x = jax.random.normal(ks[0], (B, T, D), dtype=jnp.float32)
        Wq = jax.random.normal(ks[1], (D, H * DH), dtype=jnp.float32) * s
        Wk = jax.random.normal(ks[2], (D, H * DH), dtype=jnp.float32) * s
        Ws = jax.random.normal(ks[3], (D, H * E), dtype=jnp.float32) * s
        Wd = jax.random.normal(ks[4], (D, H * E), dtype=jnp.float32) * s
        Wv = jax.random.normal(ks[5], (E, D, DH), dtype=jnp.float32) * s
        Wo = jax.random.normal(ks[6], (E, DH, D), dtype=jnp.float32) * s
        return {'x': x, 'Wq': Wq, 'Wk': Wk, 'Ws': Ws, 'Wd': Wd, 'Wv': Wv, 'Wo': Wo}
    _L0_ffn_all = _L0_ffn_setup()
    _L0_ffn_in = {k: v for k, v in _L0_ffn_all.items() if k in ('Wq', 'Wk', 'Ws', 'Wd', 'Wv', 'Wo')}
    del _L0_ffn_all

    def _L1_xattn_setup():
        import jax, jax.numpy as jnp
        import numpy as np
        B, T, S, D = (4, 256, 512, 128)
        TOP_K = 32

        def _read(query, mem_state, top_k, Wq, bq, Wk, bk, Wv, bv, Wo, bo):
            b, t, d = query.shape
            s = mem_state.shape[1]
            scale = 1.0 / np.sqrt(d)
            q = query @ Wq.T + bq
            k = mem_state @ Wk.T + bk
            v = mem_state @ Wv.T + bv
            scores = jnp.einsum('btd,bsd->bts', q, k) * scale
            if top_k < s:
                vals, idx = jax.lax.top_k(scores, top_k)
                b_ix = jnp.arange(b)[:, None, None]
                t_ix = jnp.arange(t)[None, :, None]
                masked = jnp.full_like(scores, -jnp.inf)
                scores = masked.at[b_ix, t_ix, idx].set(vals)
            attn = jax.nn.softmax(scores, axis=-1)
            ctx = jnp.einsum('bts,bsd->btd', attn, v)
            return ctx @ Wo.T + bo
        key = jax.random.key(seed)
        ks = jax.random.split(key, 12)
        std = 0.02
        inp = {'query': jax.random.normal(ks[0], (B, T, D), dtype=jnp.float32), 'mem_state': jax.random.normal(ks[1], (B, S, D), dtype=jnp.float32), 'top_k': TOP_K, 'Wq': jax.random.normal(ks[2], (D, D), dtype=jnp.float32) * std, 'bq': jnp.zeros((D,), dtype=jnp.float32), 'Wk': jax.random.normal(ks[3], (D, D), dtype=jnp.float32) * std, 'bk': jnp.zeros((D,), dtype=jnp.float32), 'Wv': jax.random.normal(ks[4], (D, D), dtype=jnp.float32) * std, 'bv': jnp.zeros((D,), dtype=jnp.float32), 'Wo': jax.random.normal(ks[5], (D, D), dtype=jnp.float32) * std, 'bo': jnp.zeros((D,), dtype=jnp.float32)}
        return inp
    _L1_xattn_all = _L1_xattn_setup()
    _L1_xattn_in = {k: v for k, v in _L1_xattn_all.items() if k in ('Wq', 'bq', 'Wk', 'bk', 'Wv', 'bv', 'Wo', 'bo')}
    del _L1_xattn_all

    def _L1_ffn_setup():
        import jax, jax.numpy as jnp
        import numpy as np
        N_HEADS = 16
        N_KV_HEADS = 4
        N_EMBD = 128
        HEAD_DIM = N_EMBD // N_HEADS
        N_EXPERTS = 8
        TOP_K = 2
        EPS = 1e-06

        def _rmsnorm(x, w):
            xf = x.astype(jnp.float32)
            n = xf * jax.lax.rsqrt(jnp.mean(xf * xf, axis=-1, keepdims=True) + EPS)
            return n.astype(x.dtype) * w

        def _gqa(x, wq, wk, wv, wo):
            B, S, C = x.shape
            n_rep = N_HEADS // N_KV_HEADS
            q = (x @ wq.T).reshape(B, S, N_HEADS, HEAD_DIM)
            k = (x @ wk.T).reshape(B, S, N_KV_HEADS, HEAD_DIM)
            v = (x @ wv.T).reshape(B, S, N_KV_HEADS, HEAD_DIM)
            k = jnp.repeat(k, n_rep, axis=2)
            v = jnp.repeat(v, n_rep, axis=2)
            scale = 1.0 / np.sqrt(HEAD_DIM).astype(np.float32)
            attn = jnp.einsum('bqhd,bkhd->bhqk', q, k) * scale
            causal = jnp.tril(jnp.ones((S, S), dtype=bool))
            attn = jnp.where(causal, attn, jnp.float32(-jnp.inf))
            attn = jax.nn.softmax(attn, axis=-1)
            out = jnp.einsum('bhqk,bkhd->bqhd', attn, v).reshape(B, S, C)
            return out @ wo.T

        def _moe(x, gate_w, expert_w):
            B, S, C = x.shape
            t = x.reshape(B * S, C)
            logits = t @ gate_w.T
            w, sel = jax.lax.top_k(logits, TOP_K)
            w = jax.nn.softmax(w.astype(jnp.float32), axis=1).astype(t.dtype)
            comb = jnp.sum(w[..., None] * jax.nn.one_hot(sel, N_EXPERTS, dtype=t.dtype), axis=1)
            out = jnp.zeros_like(t)
            for e in range(N_EXPERTS):
                out = out + comb[:, e, None] * (t @ expert_w[e].T)
            return out.reshape(B, S, C)
        key = jax.random.key(seed)
        ks = jax.random.split(key, 10)
        B, S, C = (4, 256, N_EMBD)
        s = 0.02
        return {'x': jax.random.normal(ks[0], (B, S, C), dtype=jnp.float32), 'attn_norm_w': jnp.ones((C,), dtype=jnp.float32), 'ffn_norm_w': jnp.ones((C,), dtype=jnp.float32), 'wq': jax.random.normal(ks[1], (C, C), dtype=jnp.float32) * s, 'wk': jax.random.normal(ks[2], (N_KV_HEADS * HEAD_DIM, C), dtype=jnp.float32) * s, 'wv': jax.random.normal(ks[3], (N_KV_HEADS * HEAD_DIM, C), dtype=jnp.float32) * s, 'wo': jax.random.normal(ks[4], (C, C), dtype=jnp.float32) * s, 'gate_w': jax.random.normal(ks[5], (N_EXPERTS, C), dtype=jnp.float32) * s, 'expert_w': jax.random.normal(ks[6], (N_EXPERTS, C, C), dtype=jnp.float32) * s}
    _L1_ffn_all = _L1_ffn_setup()
    _L1_ffn_in = {k: v for k, v in _L1_ffn_all.items() if k in ('attn_norm_w', 'ffn_norm_w', 'wq', 'wk', 'wv', 'wo', 'gate_w', 'expert_w')}
    del _L1_ffn_all

    def _L2_xattn_setup():
        import jax, jax.numpy as jnp
        import numpy as np
        key = jax.random.key(seed)
        k1, k2 = jax.random.split(key)
        hidden_states = jax.random.normal(k1, (8, 512, 128), dtype=jnp.float32)
        visual_hidden_state = jax.random.normal(k2, (8, 128, 128), dtype=jnp.float32)
        return {'hidden_states': hidden_states, 'visual_hidden_state': visual_hidden_state}
    _L2_xattn_all = _L2_xattn_setup()
    _L2_xattn_in = {k: v for k, v in _L2_xattn_all.items() if k in ()}
    del _L2_xattn_all

    def _L2_ffn_setup():
        import jax, jax.numpy as jnp
        import numpy as np
        QMAX = 127.0

        def _ste_round(v):
            return v + jax.lax.stop_gradient(jnp.round(v) - v)

        def _act_fake_quant(x, clip_factor):
            scale = jax.nn.sigmoid(clip_factor) * jnp.max(jnp.abs(x)) / QMAX
            return jnp.clip(_ste_round(x / scale), -QMAX - 1.0, QMAX) * scale

        def _weight_fake_quant(w):
            scale = jnp.max(jnp.abs(w), axis=1, keepdims=True) / QMAX
            return jnp.clip(_ste_round(w / scale), -QMAX - 1.0, QMAX) * scale
        key = jax.random.key(seed)
        k1, k2, k3, k4 = jax.random.split(key, 4)
        B, S, H, I = (8, 1024, 128, 352)
        return {'x': jax.random.normal(k1, (B, S, H), dtype=jnp.float32), 'clip_x': jnp.full((1,), 4.0, dtype=jnp.float32), 'clip_down': jnp.full((1,), 4.0, dtype=jnp.float32), 'w_gate': jax.random.normal(k2, (I, H), dtype=jnp.float32) * 0.02, 'w_up': jax.random.normal(k3, (I, H), dtype=jnp.float32) * 0.02, 'w_down': jax.random.normal(k4, (H, I), dtype=jnp.float32) * 0.02}
    _L2_ffn_all = _L2_ffn_setup()
    _L2_ffn_in = {k: v for k, v in _L2_ffn_all.items() if k in ('clip_x', 'clip_down', 'w_gate', 'w_up', 'w_down')}
    del _L2_ffn_all

    def _L3_xattn_setup():
        import jax, jax.numpy as jnp
        import numpy as np
        D_MODEL = 128
        NUM_HEADS = 16
        HEAD_DIM = D_MODEL // NUM_HEADS
        B, T = (4, 256)
        key = jax.random.key(seed)
        ks = jax.random.split(key, 6)
        s = 1.0 / np.sqrt(D_MODEL)
        return {'x_q': jax.random.normal(ks[0], (B, T, D_MODEL), jnp.float32), 'x_kv': jax.random.normal(ks[1], (B, T, D_MODEL), jnp.float32), 'Wq': jax.random.uniform(ks[2], (D_MODEL, D_MODEL), jnp.float32, -s, s), 'Wk': jax.random.uniform(ks[3], (D_MODEL, D_MODEL), jnp.float32, -s, s), 'Wv': jax.random.uniform(ks[4], (D_MODEL, D_MODEL), jnp.float32, -s, s), 'Wo': jax.random.uniform(ks[5], (D_MODEL, D_MODEL), jnp.float32, -s, s)}
    _L3_xattn_all = _L3_xattn_setup()
    _L3_xattn_in = {k: v for k, v in _L3_xattn_all.items() if k in ('Wq', 'Wk', 'Wv', 'Wo')}
    del _L3_xattn_all

    def _L3_ffn_setup():
        import jax, jax.numpy as jnp
        import numpy as np
        B, S, D = (4, 256, 128)
        N_EXPERTS, EXPERT_SIZE = (16, 32)
        WIDTH = N_EXPERTS * EXPERT_SIZE
        key = jax.random.key(seed)
        k_x, k_w1, k_w2, k_g = jax.random.split(key, 4)
        x = jax.random.normal(k_x, (B, S, D), dtype=jnp.float32)
        w1 = jax.random.normal(k_w1, (D, WIDTH), dtype=jnp.float32) / np.sqrt(D).astype(np.float32)
        b1 = jnp.zeros((WIDTH,), dtype=jnp.float32)
        w2 = jax.random.normal(k_w2, (WIDTH, D), dtype=jnp.float32) / np.sqrt(WIDTH).astype(np.float32)
        b2 = jnp.zeros((D,), dtype=jnp.float32)
        return {'x': x, 'w1': w1, 'b1': b1, 'w2': w2, 'b2': b2}
    _L3_ffn_all = _L3_ffn_setup()
    _L3_ffn_in = {k: v for k, v in _L3_ffn_all.items() if k in ('w1', 'b1', 'w2', 'b2')}
    del _L3_ffn_all
    return {'x': x, 'ctx_1024': ctx_1024, 'L0_xattn_Wq': _L0_xattn_in['Wq'], 'L0_xattn_bq': _L0_xattn_in['bq'], 'L0_xattn_Wk': _L0_xattn_in['Wk'], 'L0_xattn_bk': _L0_xattn_in['bk'], 'L0_xattn_Wv': _L0_xattn_in['Wv'], 'L0_xattn_bv': _L0_xattn_in['bv'], 'L0_xattn_Wo': _L0_xattn_in['Wo'], 'L0_xattn_bo': _L0_xattn_in['bo'], 'L0_ffn_Wq': _L0_ffn_in['Wq'], 'L0_ffn_Wk': _L0_ffn_in['Wk'], 'L0_ffn_Ws': _L0_ffn_in['Ws'], 'L0_ffn_Wd': _L0_ffn_in['Wd'], 'L0_ffn_Wv': _L0_ffn_in['Wv'], 'L0_ffn_Wo': _L0_ffn_in['Wo'], 'L1_xattn_Wq': _L1_xattn_in['Wq'], 'L1_xattn_bq': _L1_xattn_in['bq'], 'L1_xattn_Wk': _L1_xattn_in['Wk'], 'L1_xattn_bk': _L1_xattn_in['bk'], 'L1_xattn_Wv': _L1_xattn_in['Wv'], 'L1_xattn_bv': _L1_xattn_in['bv'], 'L1_xattn_Wo': _L1_xattn_in['Wo'], 'L1_xattn_bo': _L1_xattn_in['bo'], 'L1_ffn_attn_norm_w': _L1_ffn_in['attn_norm_w'], 'L1_ffn_ffn_norm_w': _L1_ffn_in['ffn_norm_w'], 'L1_ffn_wq': _L1_ffn_in['wq'], 'L1_ffn_wk': _L1_ffn_in['wk'], 'L1_ffn_wv': _L1_ffn_in['wv'], 'L1_ffn_wo': _L1_ffn_in['wo'], 'L1_ffn_gate_w': _L1_ffn_in['gate_w'], 'L1_ffn_expert_w': _L1_ffn_in['expert_w'], 'L2_ffn_clip_x': _L2_ffn_in['clip_x'], 'L2_ffn_clip_down': _L2_ffn_in['clip_down'], 'L2_ffn_w_gate': _L2_ffn_in['w_gate'], 'L2_ffn_w_up': _L2_ffn_in['w_up'], 'L2_ffn_w_down': _L2_ffn_in['w_down'], 'L3_xattn_Wq': _L3_xattn_in['Wq'], 'L3_xattn_Wk': _L3_xattn_in['Wk'], 'L3_xattn_Wv': _L3_xattn_in['Wv'], 'L3_xattn_Wo': _L3_xattn_in['Wo'], 'L3_ffn_w1': _L3_ffn_in['w1'], 'L3_ffn_b1': _L3_ffn_in['b1'], 'L3_ffn_w2': _L3_ffn_in['w2'], 'L3_ffn_b2': _L3_ffn_in['b2']}

def reference(x, ctx_1024, L0_xattn_Wq, L0_xattn_bq, L0_xattn_Wk, L0_xattn_bk, L0_xattn_Wv, L0_xattn_bv, L0_xattn_Wo, L0_xattn_bo, L0_ffn_Wq, L0_ffn_Wk, L0_ffn_Ws, L0_ffn_Wd, L0_ffn_Wv, L0_ffn_Wo, L1_xattn_Wq, L1_xattn_bq, L1_xattn_Wk, L1_xattn_bk, L1_xattn_Wv, L1_xattn_bv, L1_xattn_Wo, L1_xattn_bo, L1_ffn_attn_norm_w, L1_ffn_ffn_norm_w, L1_ffn_wq, L1_ffn_wk, L1_ffn_wv, L1_ffn_wo, L1_ffn_gate_w, L1_ffn_expert_w, L2_ffn_clip_x, L2_ffn_clip_down, L2_ffn_w_gate, L2_ffn_w_up, L2_ffn_w_down, L3_xattn_Wq, L3_xattn_Wk, L3_xattn_Wv, L3_xattn_Wo, L3_ffn_w1, L3_ffn_b1, L3_ffn_w2, L3_ffn_b2):
    import jax
    import jax.numpy as jnp

    def _L0_xattn_ref(queries, keys, values, Wq, bq, Wk, bk, Wv, bv, Wo, bo):
        import jax, jax.numpy as jnp
        import numpy as np
        import math
        D_MODEL = 128
        N_HEADS = 16
        D_HEAD = D_MODEL // N_HEADS
        N, L, _ = queries.shape
        S = keys.shape[1]
        H, D = (N_HEADS, D_HEAD)
        q = (queries @ Wq + bq).reshape(N, L, H, D)
        k = (keys @ Wk + bk).reshape(N, S, H, D)
        v = (values @ Wv + bv).reshape(N, S, H, D)
        sm = jnp.einsum('nlhd,nshd->nlhs', q, k) / math.sqrt(D)
        sm = jax.nn.softmax(sm, axis=1)
        attn = jnp.einsum('nlhs,nshd->nlhd', sm, v).reshape(N, L, H * D)
        return attn @ Wo + bo

    def _L0_ffn_ref(x, Wq, Wk, Ws, Wd, Wv, Wo):
        import jax, jax.numpy as jnp
        import numpy as np
        B, T, D = (4, 256, 128)
        H, DH, E, SEL = (8, 64, 5, 2)

        def _topk_mask(logits, k):
            _, idx = jax.lax.top_k(logits, k)
            return jnp.sum(jax.nn.one_hot(idx, logits.shape[-1], dtype=logits.dtype), axis=-2)
        e, d, dh = Wv.shape
        h = Wq.shape[1] // dh
        b, t, _ = x.shape
        scale = dh ** (-0.5)
        q = (x @ Wq).reshape(b, t, h, dh).transpose(0, 2, 1, 3)
        k = (x @ Wk).reshape(b, t, h, dh).transpose(0, 2, 1, 3)
        gl_v = (x @ Ws).reshape(b, t, h, e)
        wv = _topk_mask(gl_v, SEL) * jax.nn.sigmoid(gl_v)
        xv = jnp.einsum('btd,edk->btek', x, Wv)
        v = jnp.einsum('bthe,btek->bhtk', wv, xv)
        scores = jnp.einsum('bhid,bhjd->bhij', q * scale, k)
        probs = jax.nn.softmax(scores, axis=-1)
        attn = jnp.einsum('bhij,bhjd->bihd', probs, v)
        gl_o = (x @ Wd).reshape(b, t, h, e)
        mask_o = _topk_mask(gl_o, SEL)
        out = jnp.einsum('bthe,bthk,ekd->btd', mask_o, attn, Wo)
        return out

    def _L1_xattn_ref(query, mem_state, top_k, Wq, bq, Wk, bk, Wv, bv, Wo, bo):
        import jax, jax.numpy as jnp
        import numpy as np
        B, T, S, D = (4, 256, 512, 128)
        TOP_K = 32

        def _read(query, mem_state, top_k, Wq, bq, Wk, bk, Wv, bv, Wo, bo):
            b, t, d = query.shape
            s = mem_state.shape[1]
            scale = 1.0 / np.sqrt(d)
            q = query @ Wq.T + bq
            k = mem_state @ Wk.T + bk
            v = mem_state @ Wv.T + bv
            scores = jnp.einsum('btd,bsd->bts', q, k) * scale
            if top_k < s:
                vals, idx = jax.lax.top_k(scores, top_k)
                b_ix = jnp.arange(b)[:, None, None]
                t_ix = jnp.arange(t)[None, :, None]
                masked = jnp.full_like(scores, -jnp.inf)
                scores = masked.at[b_ix, t_ix, idx].set(vals)
            attn = jax.nn.softmax(scores, axis=-1)
            ctx = jnp.einsum('bts,bsd->btd', attn, v)
            return ctx @ Wo.T + bo
        return _read(query, mem_state, top_k, Wq, bq, Wk, bk, Wv, bv, Wo, bo)

    def _L1_ffn_ref(x, attn_norm_w, ffn_norm_w, wq, wk, wv, wo, gate_w, expert_w):
        import jax, jax.numpy as jnp
        import numpy as np
        N_HEADS = 16
        N_KV_HEADS = 4
        N_EMBD = 128
        HEAD_DIM = N_EMBD // N_HEADS
        N_EXPERTS = 8
        TOP_K = 2
        EPS = 1e-06

        def _rmsnorm(x, w):
            xf = x.astype(jnp.float32)
            n = xf * jax.lax.rsqrt(jnp.mean(xf * xf, axis=-1, keepdims=True) + EPS)
            return n.astype(x.dtype) * w

        def _gqa(x, wq, wk, wv, wo):
            B, S, C = x.shape
            n_rep = N_HEADS // N_KV_HEADS
            q = (x @ wq.T).reshape(B, S, N_HEADS, HEAD_DIM)
            k = (x @ wk.T).reshape(B, S, N_KV_HEADS, HEAD_DIM)
            v = (x @ wv.T).reshape(B, S, N_KV_HEADS, HEAD_DIM)
            k = jnp.repeat(k, n_rep, axis=2)
            v = jnp.repeat(v, n_rep, axis=2)
            scale = 1.0 / np.sqrt(HEAD_DIM).astype(np.float32)
            attn = jnp.einsum('bqhd,bkhd->bhqk', q, k) * scale
            causal = jnp.tril(jnp.ones((S, S), dtype=bool))
            attn = jnp.where(causal, attn, jnp.float32(-jnp.inf))
            attn = jax.nn.softmax(attn, axis=-1)
            out = jnp.einsum('bhqk,bkhd->bqhd', attn, v).reshape(B, S, C)
            return out @ wo.T

        def _moe(x, gate_w, expert_w):
            B, S, C = x.shape
            t = x.reshape(B * S, C)
            logits = t @ gate_w.T
            w, sel = jax.lax.top_k(logits, TOP_K)
            w = jax.nn.softmax(w.astype(jnp.float32), axis=1).astype(t.dtype)
            comb = jnp.sum(w[..., None] * jax.nn.one_hot(sel, N_EXPERTS, dtype=t.dtype), axis=1)
            out = jnp.zeros_like(t)
            for e in range(N_EXPERTS):
                out = out + comb[:, e, None] * (t @ expert_w[e].T)
            return out.reshape(B, S, C)
        h = x + _gqa(_rmsnorm(x, attn_norm_w), wq, wk, wv, wo)
        out = h + _moe(_rmsnorm(h, ffn_norm_w), gate_w, expert_w)
        return out

    def _L2_xattn_ref(hidden_states, visual_hidden_state):
        import jax, jax.numpy as jnp
        import numpy as np
        fusion_scores = jnp.einsum('bsd,bvd->bsv', hidden_states, visual_hidden_state)
        fusion_probs = jax.nn.softmax(fusion_scores, axis=-1)
        fusion_output = jnp.einsum('bsv,bvd->bsd', fusion_probs, visual_hidden_state)
        return fusion_output

    def _L2_ffn_ref(x, clip_x, clip_down, w_gate, w_up, w_down):
        import jax, jax.numpy as jnp
        import numpy as np
        QMAX = 127.0

        def _ste_round(v):
            return v + jax.lax.stop_gradient(jnp.round(v) - v)

        def _act_fake_quant(x, clip_factor):
            scale = jax.nn.sigmoid(clip_factor) * jnp.max(jnp.abs(x)) / QMAX
            return jnp.clip(_ste_round(x / scale), -QMAX - 1.0, QMAX) * scale

        def _weight_fake_quant(w):
            scale = jnp.max(jnp.abs(w), axis=1, keepdims=True) / QMAX
            return jnp.clip(_ste_round(w / scale), -QMAX - 1.0, QMAX) * scale
        xq = _act_fake_quant(x, clip_x[0])
        gate = jnp.einsum('bsh,ih->bsi', xq, _weight_fake_quant(w_gate))
        up = jnp.einsum('bsh,ih->bsi', xq, _weight_fake_quant(w_up))
        h = _act_fake_quant(jax.nn.silu(gate) * up, clip_down[0])
        return jnp.einsum('bsi,hi->bsh', h, _weight_fake_quant(w_down))

    def _L3_xattn_ref(x_q, x_kv, Wq, Wk, Wv, Wo):
        import jax, jax.numpy as jnp
        import numpy as np
        D_MODEL = 128
        NUM_HEADS = 16
        HEAD_DIM = D_MODEL // NUM_HEADS
        B, T = (4, 256)
        Bq, Tq, C = x_q.shape
        Tk = x_kv.shape[1]
        q = (x_q @ Wq.T).reshape(Bq, Tq, NUM_HEADS, HEAD_DIM).transpose(0, 2, 1, 3)
        k = (x_kv @ Wk.T).reshape(Bq, Tk, NUM_HEADS, HEAD_DIM).transpose(0, 2, 1, 3)
        v = (x_kv @ Wv.T).reshape(Bq, Tk, NUM_HEADS, HEAD_DIM).transpose(0, 2, 1, 3)
        scores = jnp.einsum('bhqd,bhkd->bhqk', q, k) / jnp.sqrt(jnp.asarray(HEAD_DIM, x_q.dtype))
        causal = jnp.triu(jnp.ones((Tq, Tk), bool), k=1)
        scores = jnp.where(causal, -jnp.inf, scores)
        attn = jax.nn.softmax(scores, axis=-1)
        out = jnp.einsum('bhqk,bhkd->bhqd', attn, v)
        out = out.transpose(0, 2, 1, 3).reshape(Bq, Tq, C)
        return out @ Wo.T

    def _L3_ffn_ref(x, w1, b1, w2, b2):
        import jax, jax.numpy as jnp
        import numpy as np
        B, S, D = (4, 256, 128)
        N_EXPERTS, EXPERT_SIZE = (16, 32)
        WIDTH = N_EXPERTS * EXPERT_SIZE
        h = jax.nn.relu(jnp.einsum('bsd,dw->bsw', x, w1) + b1)
        return jnp.einsum('bsw,wd->bsd', h, w2) + b2
    x = x + _L0_xattn_ref(_layernorm(x, axis=-1), ctx_1024, ctx_1024, L0_xattn_Wq, L0_xattn_bq, L0_xattn_Wk, L0_xattn_bk, L0_xattn_Wv, L0_xattn_bv, L0_xattn_Wo, L0_xattn_bo)
    x = x + _L0_ffn_ref(_layernorm(x, axis=-1), L0_ffn_Wq, L0_ffn_Wk, L0_ffn_Ws, L0_ffn_Wd, L0_ffn_Wv, L0_ffn_Wo)
    x = x + _L1_xattn_ref(_layernorm(x, axis=-1), ctx_1024, 32, L1_xattn_Wq, L1_xattn_bq, L1_xattn_Wk, L1_xattn_bk, L1_xattn_Wv, L1_xattn_bv, L1_xattn_Wo, L1_xattn_bo)
    x = x + _L1_ffn_ref(_layernorm(x, axis=-1), L1_ffn_attn_norm_w, L1_ffn_ffn_norm_w, L1_ffn_wq, L1_ffn_wk, L1_ffn_wv, L1_ffn_wo, L1_ffn_gate_w, L1_ffn_expert_w)
    x = x + _L2_xattn_ref(_layernorm(x, axis=-1), ctx_1024)
    x = x + _L2_ffn_ref(_layernorm(x, axis=-1), L2_ffn_clip_x, L2_ffn_clip_down, L2_ffn_w_gate, L2_ffn_w_up, L2_ffn_w_down)
    x = x + _L3_xattn_ref(_layernorm(x, axis=-1), ctx_1024, L3_xattn_Wq, L3_xattn_Wk, L3_xattn_Wv, L3_xattn_Wo)
    x = x + _L3_ffn_ref(_layernorm(x, axis=-1), L3_ffn_w1, L3_ffn_b1, L3_ffn_w2, L3_ffn_b2)
    return x

_drawn_inputs = setup_inputs


def setup_inputs(seed=0):
    import zlib

    import numpy as np

    out = dict(_drawn_inputs(seed))
    spreads = {'L0_xattn_bq': (0.0, 2.0),
     'L0_xattn_bk': (0.0, 0.1),
     'L0_xattn_bv': (0.0, 0.1),
     'L0_xattn_bo': (0.0, 0.1),
     'L1_xattn_bq': (0.0, 0.8),
     'L1_xattn_bk': (0.0, 2.0),
     'L1_xattn_bv': (0.0, 0.1),
     'L1_xattn_bo': (0.0, 0.1),
     'L1_ffn_attn_norm_w': (1.0, 0.6),
     'L1_ffn_ffn_norm_w': (1.0, 0.2),
     'L3_ffn_b1': (0.0, 0.794),
     'L3_ffn_b2': (0.0, 0.584)}
    factors = {'L0_ffn_Wq': 8.0,
     'L0_ffn_Wk': 8.0,
     'L0_ffn_Ws': 3.212,
     'L1_xattn_Wq': 3.522,
     'L1_xattn_Wk': 3.325,
     'L1_ffn_wq': 8.0,
     'L1_ffn_wk': 8.0,
     'L1_ffn_wv': 3.256,
     'L1_ffn_wo': 3.354,
     'L2_ffn_w_gate': 8.0,
     'L2_ffn_w_up': 8.0,
     'L2_ffn_w_down': 8.0,
     'L3_xattn_Wq': 5.613,
     'L3_xattn_Wk': 5.664}
    for name, (base, spread) in spreads.items():
        noise = np.random.default_rng([zlib.crc32(name.encode()), seed]).standard_normal(out[name].shape)
        drawn = base * np.exp(spread * noise) if base else spread * noise
        out[name] = jnp.asarray(drawn.astype(out[name].dtype))
    for name, factor in factors.items():
        out[name] = (out[name] * factor).astype(out[name].dtype)
    return out
```

```python
import concourse.bass as bass
from concourse import mybir
from contextlib import ExitStack

FP32 = mybir.dt.float32
BF16 = mybir.dt.bfloat16
ACT = mybir.ActivationFunctionType
ALU = mybir.AluOpType
X = mybir.AxisListType.X

BATCH, TOK, CH, CTX = 32, 128, 128, 77
GROUP = 4
NGROUPS = BATCH // GROUP
HEADS, HDIM = 16, 8
QUADS, SUBS = 4, 4
SH, SHD, SE = 8, 64, 5
ME = 8
INNER = 352
ITILES = [(0, 128), (128, 128), (256, 96)]
WIDTH = 512
TOPK = 32
BIG = 1.0e30
ROUND = 12582912.0
QMAX = 127.0
LN_EPS, RMS_EPS = 1e-5, 1e-6
LAG_T, LAG_V = 3, 5
POOL_OUT = 2
NCONST = 18


class Counts:

    def __init__(self):
        self.section, self.given, self.waited, self.seen = None, {}, {}, {}

    def give(self, sem):
        key = self.section, sem.name
        self.given[key] = self.given.get(key, 0) + 1
        return sem

    def at(self, sem, n):
        key = self.section, sem.name
        self.waited[key] = max(self.waited.get(key, 0), n)
        return n

    def next(self, sem):
        key = self.section, sem.name
        self.seen[key] = self.seen.get(key, 0) + 1
        return self.at(sem, self.seen[key])

    def last(self, sem):
        return self.at(sem, self.given[self.section, sem.name])

    def settle(self, eng, sem, n=None):
        key = self.section, sem.name
        n = self.waited[key] if n is None else n
        self.waited[key] = n
        eng.sem_inc(sem, -n)

    def check(self):
        assert self.given == self.waited, {k: (self.given.get(k), self.waited.get(k))
                                           for k in {*self.given, *self.waited}
                                           if self.given.get(k) != self.waited.get(k)}


class Ring:

    def __init__(self, banks, full, drained):
        self.banks, self.full, self.drained, self.taken, self.bank = banks, full, drained, 0, None

    def take(self):
        self.bank = self.banks[self.taken % len(self.banks)]
        self.taken += 1
        return self.taken

    def item(self):
        return self.taken + len(self.banks)


def four_layers(nc, d, out):
    ctx = ExitStack()
    with ctx:
        def sb(name, shape, dt=FP32):
            return ctx.enter_context(nc.sbuf_tensor(name, shape, dt))

        def sem(name):
            return ctx.enter_context(nc.semaphore(name))

        ident = sb("ident", [128, 128])
        identb = sb("identb", [128, 128], BF16)
        causal = sb("causal", [128, 4, 128], BF16)
        diag = sb("diag", [128, SUBS, QUADS])
        subone = sb("subone", [128, SUBS])
        subscale = sb("subscale", [128, SUBS])
        headsel = sb("headsel", [16, 128])
        rank5 = sb("rank5", [128, 64, SE])
        rank8 = sb("rank8", [128, GROUP, ME])
        minushalf = sb("minushalf", [128, GROUP])

        w0q, w0k, w0v, w0o = (sb(f"w0{n}", [128, 128]) for n in "qkvo")
        b0q, b0k = (sb(f"b0{n}", [128, 1]) for n in "qk")
        b0v, b0o = (sb(f"b0{n}", [128, 128]) for n in "vo")
        wsq, wsk = (sb(f"ws{n}", [128, SH * SHD]) for n in "qk")
        NV, NGATE = SE * SHD, SH * SE
        wsv = sb("wsv", [128, NV + 2 * NGATE])
        wso = sb("wso", [128, 3, 128])
        w1q, w1k, w1v, w1o = (sb(f"w1{n}", [128, 128]) for n in "qkvo")
        b1q, b1k, b1v = (sb(f"b1{n}", [128, 1]) for n in "qkv")
        b1o = sb("b1o", [128, 128])
        wgq, wgk, wgv, wgo = (sb(f"wg{n}", [128, m]) for n, m in (("q", 128), ("k", 128), ("v", 32), ("o", 128)))
        attn_w, ffn_w = sb("attn_w", [128, 1]), sb("ffn_w", [128, 1])
        wgate = sb("wgate", [128, ME])
        wexp = sb("wexp", [128, ME * 128])
        w3q, w3k, w3v, w3o = (sb(f"w3{n}", [128, 128]) for n in "qkvo")
        w31 = sb("w31", [128, WIDTH])
        b31 = sb("b31", [128, 4])
        w32 = sb("w32", [128, 4, 128])
        b32 = sb("b32", [128, 128])
        clips = sb("clips", [128, 2])
        wraw = sb("wraw", [128, 2, 3, 128])
        wdraw = sb("wdraw", [128, INNER])
        wgu = sb("wgu", [128, 2, 3 * 128], BF16)
        wdq = sb("wdq", [128, 3, 128], BF16)
        wscale = sb("wscale", [128, 2, 3])
        dscale = sb("dscale", [128, 1])
        dscaleB = sb("dscaleB", [128, 128])
        actscale = sb("actscale", [128, 8])
        ainv = sb("ainv", [128, 2])
        upscale = sb("upscale", [128, 3])
        winv = sb("winv", [128, 2, 3])
        clipe = sb("clipe", [128, 2])
        sigm = sb("sigm", [128, 2])

        x_all = sb("x_all", [128, BATCH, CH])
        ctxin = sb("ctxin", [CTX, GROUP, CH])
        nT_all = sb("nT_all", [128, BATCH * TOK])
        h_all = sb("h_all", [128, 3, BATCH * TOK])
        xg = sb("xg", [128, GROUP, CH])
        ctxg = sb("ctxg", [CTX, GROUP, CH])
        ctxT = sb("ctxT", [128, GROUP, CTX])
        n = sb("n", [128, GROUP, CH])
        nT = sb("nT", [128, GROUP * TOK])
        stats = sb("stats", [128, GROUP, 6])
        mv = sb("mv", [128, GROUP, 2])
        msq = sb("msq", [128, GROUP])
        rstd = sb("rstd", [128, GROUP])
        quad_rows = sb("quad_rows", [128, GROUP, QUADS, 128])
        sub_rows = sb("sub_rows", [128, GROUP, SUBS, 128])
        vdiag = sb("vdiag", [128, GROUP, QUADS, 160])
        vg = sb("vg", [128, GROUP, CH])
        e = sb("e", [128, 8, 512])
        eT = sb("eT", [128, 4, 512])
        negmax = sb("negmax", [128, GROUP, 16])
        zsum = sb("zsum", [128, GROUP, 16])
        rz = sb("rz", [128, GROUP, 16])
        rzT = sb("rzT", [16, GROUP * TOK])
        rzB = sb("rzB", [128, GROUP * TOK])
        aT = sb("aT", [128, GROUP * TOK])
        tsel = sb("tsel", [128, 4, 64 * SE])
        tm = sb("tm", [128, 4, 64])
        gates = sb("gates", [128, GROUP, 2 * SH, SE])
        gexp = sb("gexp", [128, GROUP, SH, SE])
        top8 = sb("top8", [128, GROUP, 4, 8])
        work = sb("work", [128, GROUP, CTX])
        sc = sb("sc", [128, GROUP, CTX])
        z1 = sb("z1", [128, GROUP])
        hres = sb("hres", [128, GROUP, CH])
        comb = sb("comb", [128, GROUP, ME])
        clog = sb("clog", [128, GROUP, ME])
        amax = sb("amax", [128, NGROUPS])
        hmax = sb("hmax", [128, 3 * NGROUPS])
        gmax = sb("gmax", [128, 4])
        hf = h_all[:, :, :].rearrange("p a b -> p (a b)")
        at = [0]

        def part(size):
            at[0] += size
            return hf[:, at[0] - size:at[0]]
        qf = part(4 * 512).rearrange("p (t n) -> p t n", t=4)
        kf = sub_rows[:, :, :, :].rearrange("p b j n -> p b (j n)")
        xvs = part(GROUP * 400).rearrange("p (b n) -> p b n", b=GROUP)
        vs = part(GROUP * 512).rearrange("p (b n) -> p b n", b=GROUP)
        prod = part(2 * 512).rearrange("p (r n) -> p r n", r=2)
        av = part(GROUP * 512).rearrange("p (b n) -> p b n", b=GROUP)
        oprod = part(SE * 512).rearrange("p (e n) -> p e n", e=SE)
        ys, ysT = tsel, qf[:, 0:3, :]
        assert at[0] <= 3 * BATCH * TOK
        hq = sb("hq", [128, 3, GROUP * TOK], BF16)
        xq = sb("xq", [128, 2, GROUP * TOK], BF16)
        hid = eT
        wk32 = e[:, 2:8, :]

        banks = [ctx.enter_context(nc.psum_tensor(f"bank{i}", [128, 512], FP32)) for i in range(8)]
        A, D, SC = banks[0:2], banks[2:4], banks[4:8]

        loaded, consts = sem("loaded"), sem("consts")
        stored, x_done = sem("stored"), sem("x_done")
        a_full, a_drained = sem("a_full"), sem("a_drained")
        d_full, d_drained = sem("d_full"), sem("d_drained")
        s_full, s_drained = sem("s_full"), sem("s_drained")
        ctx_in, ctxin_free = sem("ctx_in"), sem("ctxin_free")
        xg_taken, ctx_taken, group_free = sem("xg_taken"), sem("ctx_taken"), sem("group_free")
        dve_step, pool_step = sem("dve_step"), sem("pool_step")
        var_ready, rstd_ready, n_ready = sem("var_ready"), sem("rstd_ready"), sem("n_ready")
        n_read = sem("n_read")
        max_ready, e_before = sem("max_ready"), sem("e_before")
        v_ready, e_used = sem("v_ready"), sem("e_used")
        rz_ready, rzB_ready = sem("rz_ready"), sem("rzB_ready")
        xv_ready, sig_ready, gate_ready = sem("xv_ready"), sem("sig_ready"), sem("gate_ready")
        prod_ready, prod_free = sem("prod_ready"), sem("prod_free")
        av_dve, av_pool, ogate_ready = sem("av_dve"), sem("av_pool"), sem("ogate_ready")
        oprod_ready, oprod_free, y_ready = sem("oprod_ready"), sem("oprod_free"), sem("y_ready")
        pmax_ready, pexp_ready, p_ready = sem("pmax_ready"), sem("pexp_ready"), sem("p_ready")
        c_ready, cexp_ready = sem("c_ready"), sem("cexp_ready")
        w_ready, clip_exp = sem("w_ready"), sem("clip_exp")
        amax_ready, gmax_ready, sx_ready = sem("amax_ready"), sem("gmax_ready"), sem("sx_ready")
        q_ready, sil_ready, h_done = sem("q_ready"), sem("sil_ready"), sem("h_done")

        C = Counts()
        ctx.enter_context(nc.allow_non_contiguous_dma(reason="a bias of 512 as columns, once"))
        block = ctx.enter_context(nc.Block())
        LOADS = []

        def load(dst, src):
            LOADS.append((dst, src))
        for g in range(NGROUPS):
            load(x_all[:, g * GROUP:(g + 1) * GROUP, :], d["x"][g * GROUP:(g + 1) * GROUP].rearrange("b t c -> t b c"))
            if g == 0:
                col = lambda v: v.rearrange("(p a) -> p a", a=1)
                row = lambda v: v.rearrange("(a p) -> a p", a=1).broadcast_to([128, v.shape[0]])
                for dst, name in ((w0q, "Wq"), (w0k, "Wk"), (w0v, "Wv"), (w0o, "Wo")):
                    load(dst[:], d["L0_xattn_" + name])
                load(b0q[:], col(d["L0_xattn_bq"]))
                load(b0k[:], col(d["L0_xattn_bk"]))
                load(b0v[:], row(d["L0_xattn_bv"]))
                load(b0o[:], row(d["L0_xattn_bo"]))
                load(wsq[:], d["L0_ffn_Wq"])
                load(wsk[:], d["L0_ffn_Wk"])
                load(wsv[:, 0:NV].rearrange("p (e k) -> p e k", e=SE), d["L0_ffn_Wv"].rearrange("e d k -> d e k"))
                load(wsv[:, NV:NV + NGATE], d["L0_ffn_Ws"])
                load(wsv[:, NV + NGATE:], d["L0_ffn_Wd"])
                wo = d["L0_ffn_Wo"].rearrange("e k c -> (e k) c")
                load(wso[:, 0:2, :], wo[0:256].rearrange("(t p) c -> p t c", p=128))
                load(wso[0:64, 2, :], wo[256:320])
                for dst, name in ((w1q, "Wq"), (w1k, "Wk"), (w1v, "Wv"), (w1o, "Wo")):
                    load(dst[:], d["L1_xattn_" + name])
                for dst, name in ((b1q, "bq"), (b1k, "bk"), (b1v, "bv")):
                    load(dst[:], col(d["L1_xattn_" + name]))
                load(b1o[:], row(d["L1_xattn_bo"]))
                load(wgq[:], d["L1_ffn_wq"])
                for j in range(SUBS):
                    load(wgk[:, :].rearrange("p (g j d) -> p g j d", g=QUADS, j=SUBS)[:, :, j, :],
                         d["L1_ffn_wk"].rearrange("c (g d) -> c g d", g=QUADS))
                load(wgv[:], d["L1_ffn_wv"])
                load(wgo[:], d["L1_ffn_wo"])
                load(attn_w[:], col(d["L1_ffn_attn_norm_w"]))
                load(ffn_w[:], col(d["L1_ffn_ffn_norm_w"]))
                load(wgate[:], d["L1_ffn_gate_w"])
                load(wexp[:, :].rearrange("p (e o) -> p e o", e=ME), d["L1_ffn_expert_w"].rearrange("e c o -> c e o"))
                for dst, name in ((w3q, "Wq"), (w3k, "Wk"), (w3v, "Wv"), (w3o, "Wo")):
                    load(dst[:], d["L3_xattn_" + name])
                load(w31[:], d["L3_ffn_w1"])
                load(b31[:], d["L3_ffn_b1"].rearrange("(t p) -> p t", p=128))
                load(w32[:], d["L3_ffn_w2"].rearrange("(t p) c -> p t c", p=128))
                load(b32[:], row(d["L3_ffn_b2"]))
                load(clips[:, 0:1], d["L2_ffn_clip_x"].rearrange("(a p) -> a p", a=1).broadcast_to([128, 1]))
                load(clips[:, 1:2], d["L2_ffn_clip_down"].rearrange("(a p) -> a p", a=1).broadcast_to([128, 1]))
                for w, name in ((0, "gate"), (1, "up")):
                    for t, (r0, m) in enumerate(ITILES):
                        load(wraw[0:m, w, t, :], d["L2_ffn_w_" + name][r0:r0 + m])
                load(wdraw[:], d["L2_ffn_w_down"])
        NLOAD = 16 * len(LOADS)

        @block.sync
        def _(sp):
            def load_context(it):
                sp.wait_ge(ctxin_free, C.at(ctxin_free, 1))
                sp.dma_start(ctxin[:], d["ctx_1024"][bass.ds(it * GROUP, GROUP)].rearrange("b t c -> t b c"))\
                    .then_inc(ctx_in, 16)
                C.settle(sp, ctxin_free)

            for dst, src in LOADS:
                sp.dma_start(dst, src).then_inc(loaded, 16)
            C.section = "A"
            with sp.Fori(0, NGROUPS) as it:
                load_context(it)
            C.section = "C"
            with sp.Fori(0, NGROUPS) as it:
                load_context(it)
                sp.wait_ge(x_done, C.next(x_done))
                sp.dma_start(out[bass.ds(it * GROUP, GROUP)].rearrange("b t c -> t b c"),
                             x_all[:, bass.ds(it * GROUP, GROUP), :]).then_inc(stored, 16)
                C.settle(sp, x_done)
            sp.wait_ge(stored, 16 * NGROUPS)

        @block.gpsimd
        def _(pool):
            k = [0]

            def done(ins):
                k[0] += 1
                ins.then_inc(consts, 1)
                pool.wait_ge(consts, k[0])
            done(pool.memset(quad_rows[:], 0.0))
            done(pool.memset(vdiag[:], 0.0))
            done(pool.memset(hmax[:], 0.0))
            done(pool.memset(ident[:], 0.0))
            done(pool.affine_select(out=ident[:], in_=ident[:], compare_op=ALU.not_equal, fill=1.0, base=0,
                                    pattern=[[-1, 128]], channel_multiplier=1))
            done(pool.tensor_copy(identb[:], ident[:]))
            done(pool.memset(causal[:], 0.0))
            done(pool.affine_select(out=causal[:], in_=causal[:], compare_op=ALU.is_ge, fill=-BIG, base=0,
                                    pattern=[[0, 4], [-1, 128]], channel_multiplier=1))
            done(pool.memset(diag[:], 1.0))
            done(pool.affine_select(out=diag[:], in_=diag[:], compare_op=ALU.is_ge, fill=0.0, base=0,
                                    pattern=[[-8, 4], [-32, 4]], channel_multiplier=1))
            done(pool.affine_select(out=diag[:], in_=diag[:], compare_op=ALU.is_ge, fill=0.0, base=7,
                                    pattern=[[8, 4], [32, 4]], channel_multiplier=-1))
            done(pool.tensor_tensor(subscale[:], diag[:, :, 0], diag[:, :, 1], ALU.add))
            done(pool.tensor_tensor(subone[:], diag[:, :, 2], diag[:, :, 3], ALU.add))
            done(pool.tensor_tensor(subone[:], subone[:], subscale[:], ALU.add))
            done(pool.tensor_scalar(subscale[:], subone[:], float(HDIM) ** -0.5, None, ALU.mult))
            done(pool.iota(rank5[:], pattern=[[0, 64], [-1, SE]], base=SE, channel_multiplier=0,
                           allow_small_or_imprecise_dtypes=True))
            done(pool.iota(rank8[:], pattern=[[0, GROUP], [-1, ME]], base=ME, channel_multiplier=0,
                           allow_small_or_imprecise_dtypes=True))
            done(pool.memset(minushalf[:], -0.5))
            assert k[0] == NCONST
            pool.wait_ge(loaded, NLOAD)

            def rsqrt(eps):
                pool.wait_ge(var_ready, C.next(var_ready))
                pool.tensor_scalar(rstd[:], mv[:, :, 1], eps, None, ALU.add).then_inc(C.give(pool_step), 1)
                pool.wait_ge(pool_step, C.next(pool_step))
                pool.tensor_tensor(rstd[:], rstd[:], minushalf[:], ALU.pow).then_inc(C.give(rstd_ready), 1)

            def take_group(it):
                pool.wait_ge(group_free, C.at(group_free, 1))
                pool.tensor_copy(xg[:], x_all[:, bass.ds(it * GROUP, GROUP), :]).then_inc(C.give(xg_taken), 1)
                pool.wait_ge(ctx_in, 16)
                pool.sem_inc(ctx_in, -16)
                pool.tensor_copy(ctxg[:], ctxin[:]).then_inc(C.give(ctx_taken), 1)
                pool.drain().then_inc(C.give(ctxin_free), 1)

            C.section = "A"
            with pool.Fori(0, NGROUPS) as it:
                take_group(it)
                rsqrt(LN_EPS)
                rsqrt(LN_EPS)
                pool.wait_ge(gate_ready, C.next(gate_ready))
                m = 0
                for b in range(GROUP):
                    for ex in range(SE):
                        dst = vs[:, b, :] if ex == 0 else prod[:, m % 2, :]
                        if ex:
                            pool.wait_ge(prod_free, C.at(prod_free, m + 1))
                            m += 1
                        pool.tensor_tensor(
                            dst.rearrange("p (h k) -> p h k", h=SH),
                            xvs[:, b, ex * SHD:(ex + 1) * SHD].unsqueeze(1).broadcast_to([128, SH, SHD]),
                            gates[:, b, 0:SH, ex].unsqueeze(2).broadcast_to([128, SH, SHD]),
                            ALU.mult).then_inc(C.give(prod_ready), 1)
                for b in range(GROUP):
                    pool.wait_ge(ogate_ready, C.next(ogate_ready))
                    pool.wait_ge(av_pool, C.next(av_pool))
                    pool.wait_ge(oprod_free, C.at(oprod_free, b + 1))
                    for ex in range(POOL_OUT):
                        ins = pool.tensor_tensor(
                            oprod[:, ex, :].rearrange("p (h k) -> p h k", h=SH),
                            av[:, b, :].rearrange("p (h k) -> p h k", h=SH),
                            gates[:, b, SH:, ex].unsqueeze(2).broadcast_to([128, SH, SHD]), ALU.mult)
                    ins.then_inc(C.give(oprod_ready), 1)
                rsqrt(LN_EPS)
                rsqrt(LN_EPS)
                rsqrt(RMS_EPS)
                rsqrt(RMS_EPS)
                rsqrt(LN_EPS)
                rsqrt(LN_EPS)
                for s in (group_free, var_ready, pool_step, gate_ready, ogate_ready, av_pool, oprod_free):
                    C.settle(pool, s)
                C.settle(pool, prod_free, m)
            for i in range(2):
                pool.wait_ge(amax_ready, i + 1)
                pool.partition_all_reduce(gmax[:, 2 * i + 1:2 * i + 2], gmax[:, 2 * i:2 * i + 1], 128,
                                          bass.bass_isa.ReduceOp.max).then_inc(gmax_ready, 1)
            C.section = "C"
            with pool.Fori(0, NGROUPS) as it:
                take_group(it)
                rsqrt(LN_EPS)
                rsqrt(LN_EPS)
                for s in (group_free, var_ready, pool_step):
                    C.settle(pool, s)

        @block.tensor
        def _(pe):
            pe.wait_ge(loaded, NLOAD)
            pe.wait_ge(consts, NCONST)
            ring_a, ring_d = Ring(A, a_full, a_drained), Ring(D, d_full, d_drained)
            ring_s = Ring(SC, s_full, s_drained)

            def settle(*sems):
                for ring in (ring_a, ring_d, ring_s):
                    if ring.taken:
                        assert ring.taken % len(ring.banks) == 0
                        C.settle(pe, ring.drained, ring.taken)
                        ring.taken = 0
                for s in sems:
                    C.settle(pe, s)

            mm = pe.matmul

            def tokens(b):
                return slice(b * TOK, (b + 1) * TOK)

            def transpose_n():
                pe.wait_ge(n_ready, C.next(n_ready))
                pe.wait_ge(a_drained, ring_a.take())
                o = ring_a.bank
                for b in range(GROUP):
                    ins = pe.transpose(o[:, tokens(b)], n[:, b, :], ident[:])
                ins.then_inc(C.give(a_full), 1)
                return ring_a.item()

            def transpose_ctx(items):
                pe.wait_ge(ctx_taken, C.next(ctx_taken))
                for i in range(items):
                    pe.wait_ge(a_drained, ring_a.take())
                    o = ring_a.bank
                    for b in range(GROUP // items):
                        ins = pe.transpose(o[:, b * CTX:(b + 1) * CTX], ctxg[:, i * GROUP // items + b, :],
                                           ident[0:CTX, 0:CTX])
                    ins.then_inc(C.give(a_full), 1)
                    item = ring_a.item()
                return item

            def project(ring, w, src):
                pe.wait_ge(ring.drained, ring.take())
                o = ring.bank
                mm(o[0:w.shape[1], 0:src.shape[1]], w, src, start=True, stop=True).then_inc(C.give(ring.full), 1)
                return ring.item()

            ctxT2 = ctxT[:, :, :].rearrange("p b s -> p (b s)")

            def values(ring, w, src, rows=TOK):
                pe.wait_ge(ring.drained, ring.take())
                o = ring.bank
                cols = w.shape[1]
                for b in range(GROUP):
                    ins = mm(o[0:rows, b * cols:(b + 1) * cols], src(b), w, start=True, stop=True)
                ins.then_inc(C.give(ring.full), 1)
                return ring.item()

            def heads_out(w):
                return values(ring_d, w, lambda b: aT[:, tokens(b)])

            def nTb(b):
                return nT[:, tokens(b)]

            def add_heads(o, b, j, rows, rhs):
                for g in range(QUADS):
                    ins = mm(o[32 * g:32 * g + 32, tokens(b)], vdiag[0:rows, b, g, 32 * j:32 * j + 32],
                             rhs(g), start=(j == 0), stop=(j == SUBS - 1))
                return ins

            def causal_heads(keys, q_item, k_item, v_item):
                units = [(b, j) for b in range(GROUP) for j in range(SUBS)]
                pe.wait_ge(d_drained, q_item)
                pe.wait_ge(a_drained, k_item)
                s_items, t_items = {}, {}
                o = None
                for u in range(len(units) + LAG_V):
                    if u < len(units):
                        b, j = units[u]
                        pe.wait_ge(s_drained, ring_s.take())
                        s = ring_s.bank[:, 0:4 * keys].rearrange("p (g k) -> p g k", g=QUADS)
                        mm(s, sub_rows[:, b, j, :], quad_rows[:, b, :, 0:keys], start=True, stop=False)
                        mm(s, identb[:], causal[:, :, 0:keys], start=False, stop=True).then_inc(C.give(s_full), 1)
                        s_items[u] = ring_s.item()
                    v = u - LAG_T
                    if 0 <= v < len(units):
                        pe.wait_ge(a_drained, ring_a.take())
                        t = ring_a.bank
                        pe.wait_ge(s_drained, s_items[v])
                        for g in range(QUADS):
                            ins = pe.transpose(t[0:keys, tokens(g)], e[:, v % 8, g * keys:(g + 1) * keys], ident[:])
                        ins.then_inc(C.give(a_full), 1)
                        t_items[v] = ring_a.item()
                    v = u - LAG_V
                    if 0 <= v < len(units):
                        b, j = units[v]
                        if v == 0:
                            pe.wait_ge(d_drained, ring_d.take())
                            o = ring_d.bank
                            pe.wait_ge(d_drained, v_item)
                        pe.wait_ge(a_drained, t_items[v])
                        ins = add_heads(o, b, j, keys, lambda g: eT[0:keys, v % 4, tokens(g)])
                ins.then_inc(C.give(d_full), 1)
                heads_item = ring_d.item()
                pe.wait_ge(rz_ready, C.next(rz_ready))
                pe.wait_ge(a_drained, ring_a.take())
                t = ring_a.bank
                for b in range(GROUP):
                    ins = pe.transpose(t[0:16, tokens(b)], rz[:, b, :], ident[:])
                ins.then_inc(C.give(a_full), 1)
                pe.wait_ge(a_drained, ring_a.item())
                project(ring_a, headsel[:], rzT[:])
                return heads_item

            def transpose_p():
                pe.wait_ge(p_ready, C.next(p_ready))
                pe.wait_ge(a_drained, ring_a.take())
                t = ring_a.bank
                for b in range(GROUP):
                    ins = pe.transpose(t[0:CTX, tokens(b)], work[:, b, :], ident[:])
                ins.then_inc(C.give(a_full), 1)
                return ring_a.item()

            C.section = "setup"
            for w in range(2):
                pe.wait_ge(w_ready, C.next(w_ready))
                pe.wait_ge(a_drained, ring_a.take())
                o = ring_a.bank
                for t, (r0, m) in enumerate(ITILES):
                    ins = pe.transpose(o[:, r0:r0 + m], wraw[0:m, w, t, :], ident[0:m, 0:m])
                ins.then_inc(C.give(a_full), 1)
            pe.wait_ge(w_ready, C.next(w_ready))
            pe.wait_ge(a_drained, ring_a.take())
            o = ring_a.bank
            for t, (r0, m) in enumerate(ITILES):
                pe.transpose(o[0:m, t * 128:(t + 1) * 128], wdraw[:, r0:r0 + m], ident[:])
            pe.transpose(o[0:16, 384:512], diag[:, :, :].rearrange("p j g -> p (j g)"), ident[:])\
                .then_inc(C.give(a_full), 1)
            pe.wait_ge(w_ready, C.next(w_ready))
            pe.wait_ge(a_drained, project(ring_a, dscaleB[:], ident[:]))
            settle(w_ready)

            C.section = "A"
            with pe.Fori(0, NGROUPS) as it:
                ctx_item = transpose_ctx(2)
                n_item = transpose_n()
                pe.wait_ge(a_drained, ctx_item)
                k_item = project(ring_d, w0k[:], ctxT2)
                v_item = values(ring_d, w0v[:], lambda b: ctxT[:, b, :], CTX)
                pe.wait_ge(a_drained, n_item)
                q_item = project(ring_a, w0q[:], nT[:])
                pe.wait_ge(d_drained, k_item)
                pe.wait_ge(d_drained, v_item)
                pe.wait_ge(a_drained, q_item)
                s_items = {}
                for b in range(GROUP + 1):
                    if b < GROUP:
                        for j in range(SUBS):
                            pe.wait_ge(s_drained, ring_s.take())
                            s = ring_s.bank[0:CTX, :].rearrange("p (g t) -> p g t", g=QUADS)
                            mm(s, sub_rows[:, b, j, 0:CTX], quad_rows[:, b, :, :],
                               start=True, stop=True).then_inc(C.give(s_full), 1)
                            s_items[b, j] = ring_s.item()
                    if b > 0:
                        c = b - 1
                        if c == 0:
                            pe.wait_ge(a_drained, ring_a.take())
                            o = ring_a.bank
                        pe.wait_ge(v_ready, C.next(v_ready))
                        for j in range(SUBS):
                            pe.wait_ge(s_drained, s_items[c, j])
                            ins = add_heads(o, c, j, CTX, lambda g: e[0:CTX, (4 * c + j) % 8, tokens(g)])
                        if c < 2:
                            ins.then_inc(C.give(e_used), 1)
                ins.then_inc(C.give(a_full), 1)
                pe.wait_ge(a_drained, ring_a.item())
                heads_out(w0o[:])

                pe.wait_ge(a_drained, transpose_n())
                for b in range(GROUP):
                    pe.wait_ge(a_drained, ring_a.take())
                    o = ring_a.bank
                    mm(o[:, 0:NV + 2 * NGATE], nTb(b), wsv[:], start=True, stop=True).then_inc(C.give(a_full), 1)
                for t in range(4):
                    q_item = project(ring_a, wsq[:, t * 128:(t + 1) * 128], nT[:])
                    k_item = project(ring_d, wsk[:, t * 128:(t + 1) * 128], nT[:])
                pe.wait_ge(a_drained, q_item)
                pe.wait_ge(d_drained, k_item)
                units = [(b, p) for b in range(GROUP) for p in range(2)]
                s_items, t_items = {}, {}
                for u in range(len(units) + LAG_V):
                    if u < len(units):
                        b, p = units[u]
                        pe.wait_ge(s_drained, ring_s.take())
                        s = ring_s.bank
                        for t in range(4):
                            ins = mm(s[:, tokens(t)], qf[64 * p:64 * p + 64, t, tokens(b)],
                                     kf[64 * p:64 * p + 64, t, tokens(b)], start=True, stop=True)
                        ins.then_inc(C.give(s_full), 1)
                        s_items[u] = ring_s.item()
                    v = u - LAG_T
                    if 0 <= v < len(units):
                        pe.wait_ge(a_drained, ring_a.take())
                        tb = ring_a.bank
                        pe.wait_ge(s_drained, s_items[v])
                        for t in range(4):
                            ins = pe.transpose(tb[:, tokens(t)], e[:, v % 8, tokens(t)], ident[:])
                        ins.then_inc(C.give(a_full), 1)
                        t_items[v] = ring_a.item()
                    v = u - LAG_V
                    if 0 <= v < len(units) and v % 2 == 1:
                        b = v // 2
                        pe.wait_ge(a_drained, ring_a.take())
                        o = ring_a.bank
                        pe.wait_ge(v_ready, C.next(v_ready))
                        pe.wait_ge(a_drained, t_items[v])
                        for p in range(2):
                            for t in range(4):
                                h = 2 * t + p
                                ins = mm(o[:, h * SHD:(h + 1) * SHD], eT[:, (v - 1 + p) % 4, tokens(t)],
                                         vs[:, b, h * SHD:(h + 1) * SHD], start=True, stop=True)
                        ins.then_inc(C.give(a_full), 1)
                pe.wait_ge(y_ready, C.next(y_ready))
                for t in range(3):
                    rows = min(128, NV - 128 * t)
                    pe.wait_ge(a_drained, ring_a.take())
                    tb = ring_a.bank
                    for b in range(GROUP):
                        ins = pe.transpose(tb[0:rows, tokens(b)], ys[:, b, 128 * t:128 * t + rows], ident[:])
                    ins.then_inc(C.give(a_full), 1)
                pe.wait_ge(d_drained, ring_d.take())
                o = ring_d.bank
                pe.wait_ge(a_drained, ring_a.item())
                for b in range(GROUP):
                    for t in range(3):
                        rows = min(128, NV - 128 * t)
                        ins = mm(o[:, tokens(b)], ysT[0:rows, t, tokens(b)], wso[0:rows, t, :],
                                 start=(t == 0), stop=(t == 2))
                ins.then_inc(C.give(d_full), 1)

                k_item = project(ring_a, w1k[:], ctxT2)
                v_item = values(ring_d, w1v[:], lambda b: ctxT[:, b, :], CTX)
                pe.wait_ge(a_drained, transpose_n())
                q_item = project(ring_a, w1q[:], nT[:])
                pe.wait_ge(d_drained, v_item)
                pe.wait_ge(a_drained, q_item)
                pe.wait_ge(d_drained, ring_d.take())
                o = ring_d.bank
                for b in range(GROUP):
                    ins = mm(o[:, b * CTX:(b + 1) * CTX], qf[:, 0, tokens(b)], kf[:, 0, b * CTX:(b + 1) * CTX],
                             start=True, stop=True)
                ins.then_inc(C.give(d_full), 1)
                pe.wait_ge(a_drained, transpose_p())
                pe.wait_ge(a_drained, ring_a.take())
                o = ring_a.bank
                for b in range(GROUP):
                    ins = mm(o[:, tokens(b)], vg[0:CTX, b, :], eT[0:CTX, 0, tokens(b)], start=True, stop=True)
                ins.then_inc(C.give(a_full), 1)
                pe.wait_ge(a_drained, ring_a.item())
                heads_out(w1o[:])

                pe.wait_ge(a_drained, transpose_n())
                k_item = project(ring_a, wgk[:], nT[:])
                q_item = project(ring_d, wgq[:], nT[:])
                v_item = values(ring_d, wgv[:], nTb)
                pe.wait_ge(d_drained, causal_heads(TOK, q_item, k_item, v_item))
                heads_out(wgo[:])
                pe.wait_ge(a_drained, transpose_n())
                values(ring_d, wgate[:], nTb)
                for b in range(GROUP):
                    for half in range(2):
                        pe.wait_ge(d_drained, ring_d.take())
                        o = ring_d.bank
                        mm(o[:], nTb(b), wexp[:, half * 512:(half + 1) * 512], start=True, stop=True).then_inc(C.give(d_full), 1)

                pe.wait_ge(a_drained, transpose_n())
                pe.wait_ge(d_drained, ring_d.take())
                o = ring_d.bank
                for b in range(GROUP):
                    ins = mm(o[:, b * CTX:(b + 1) * CTX], nTb(b), ctxT[:, b, :], start=True, stop=True)
                ins.then_inc(C.give(d_full), 1)
                pe.wait_ge(a_drained, transpose_p())
                pe.wait_ge(d_drained, ring_d.take())
                o = ring_d.bank
                for b in range(GROUP):
                    ins = mm(o[:, tokens(b)], eT[0:CTX, 0, tokens(b)], ctxg[:, b, :], start=True, stop=True)
                ins.then_inc(C.give(d_full), 1)
                transpose_n()
                pe.drain().then_inc(C.give(n_read), 1)
                settle(n_ready, ctx_taken, v_ready, rz_ready, y_ready, p_ready)

            C.section = "B"
            with pe.Fori(0, NGROUPS // 2) as it:
                for r in range(2):
                    pe.wait_ge(q_ready, C.next(q_ready))
                    for r0, m in ITILES:
                        project(ring_a, wgu[:, 0, r0:r0 + m], xq[:, r, :])
                        project(ring_d, wgu[:, 1, r0:r0 + m], xq[:, r, :])
                settle(q_ready)

            C.section = "C"
            with pe.Fori(0, NGROUPS) as it:
                pe.wait_ge(q_ready, C.next(q_ready))
                pe.wait_ge(d_drained, ring_d.take())
                o = ring_d.bank
                for b in range(GROUP):
                    for t, (r0, m) in enumerate(ITILES):
                        ins = mm(o[:, tokens(b)], hq[0:m, t, tokens(b)], wdq[0:m, t, :],
                                 start=(t == 0), stop=(t == 2))
                ins.then_inc(C.give(d_full), 1)
                pe.wait_ge(a_drained, transpose_ctx(1))
                k_item = project(ring_a, w3k[:], ctxT2)
                v_item = values(ring_d, w3v[:], lambda b: ctxT[:, b, :], CTX)
                pe.wait_ge(a_drained, transpose_n())
                q_item = project(ring_d, w3q[:], nT[:])
                pe.wait_ge(d_drained, causal_heads(CTX, q_item, k_item, v_item))
                heads_out(w3o[:])
                pe.wait_ge(a_drained, transpose_n())
                for t in range(4):
                    h_item = project(ring_a, w31[:, t * 128:(t + 1) * 128], nT[:])
                pe.wait_ge(a_drained, h_item)
                pe.wait_ge(d_drained, ring_d.take())
                o = ring_d.bank
                for b in range(GROUP):
                    for t in range(4):
                        ins = mm(o[:, tokens(b)], hid[:, t, tokens(b)], w32[:, t, :], start=(t == 0), stop=(t == 3))
                ins.then_inc(C.give(d_full), 1)
                settle(ctx_taken, n_ready, q_ready, rz_ready)

        @block.scalar
        def _(act):
            act.wait_ge(loaded, NLOAD)
            act.wait_ge(consts, NCONST)
            ring_a, ring_s = Ring(A, a_full, a_drained), Ring(SC, s_full, s_drained)

            def copy(dst, src, bias=0.0, scale=1.0, func=ACT.Identity):
                return act.activation(dst, src, func, bias=bias, scale=scale)

            def settle(*sems):
                if ring_a.taken:
                    C.settle(act, a_full, ring_a.taken)
                ring_a.taken = ring_s.taken = 0
                for s in sems:
                    C.settle(act, s)

            def take_n(scale=1.0):
                act.wait_ge(a_full, ring_a.take())
                copy(nT[:], ring_a.bank[:], scale=scale).then_inc(C.give(a_drained), 1)

            def take_ctx(items):
                for i in range(items):
                    k = GROUP // items
                    act.wait_ge(a_full, ring_a.take())
                    copy(ctxT[:, i * k:(i + 1) * k, :].rearrange("p b s -> p (b s)"), ring_a.bank[:, 0:k * CTX]).then_inc(C.give(a_drained), 1)

            def take_quads(cols, bias=None):
                act.wait_ge(a_full, ring_a.take())
                o = ring_a.bank
                for g in range(QUADS):
                    p = slice(32 * g, 32 * g + 32)
                    ins = copy(quad_rows[p, :, g, 0:cols], o[p, 0:GROUP * cols].rearrange("p (b t) -> p b t", b=GROUP),
                               bias=bias[p, :] if bias is not None else 0.0)
                ins.then_inc(C.give(a_drained), 1)

            def exps(rows, width, b, j, u):
                act.wait_ge(max_ready, C.next(max_ready))
                ring_s.take()
                o = ring_s.bank
                for g in range(4):
                    ins = act.activation(e[0:rows, u % 8, g * width:(g + 1) * width], o[0:rows, g * width:(g + 1) * width],
                                         ACT.Exp, bias=negmax[0:rows, b, 4 * j + g:4 * j + g + 1])
                    if g == 0:
                        ins.then_inc(C.give(e_before), 1)
                ins.then_inc(C.give(s_drained), 1)

            def last_exps_done():
                act.drain().then_inc(C.give(e_before), 1)

            def causal_heads(keys):
                n_units = GROUP * SUBS
                for u in range(n_units + LAG_T):
                    if u < n_units:
                        exps(TOK, keys, u // SUBS, u % SUBS, u)
                        if u == n_units - 1:
                            last_exps_done()
                    v = u - LAG_T
                    if 0 <= v:
                        act.wait_ge(a_full, ring_a.take())
                        copy(eT[0:keys, v % 4, :], ring_a.bank[0:keys, :]).then_inc(C.give(a_drained), 1)
                act.wait_ge(a_full, ring_a.take())
                copy(rzT[:], ring_a.bank[0:16, :]).then_inc(C.give(a_drained), 1)
                act.wait_ge(a_full, ring_a.take())
                copy(rzB[:], ring_a.bank[:]).then_inc(C.give(a_drained), 1)
                act.drain().then_inc(C.give(rzB_ready), 1)

            def exp_p(src):
                act.wait_ge(pmax_ready, C.next(pmax_ready))
                for b in range(GROUP):
                    ins = act.activation(e[:, 0, b * CTX:(b + 1) * CTX], src[:, b, :], ACT.Exp, bias=negmax[:, b, 0:1])
                ins.then_inc(C.give(pexp_ready), 1)
                act.wait_ge(a_full, ring_a.take())
                copy(eT[0:CTX, 0, :], ring_a.bank[0:CTX, :]).then_inc(C.give(a_drained), 1)

            C.section = "setup"
            act.wait_ge(a_full, ring_a.take())
            copy(wgu[:, 0, 0:INNER], ring_a.bank[:, 0:INNER]).then_inc(C.give(a_drained), 1)
            act.wait_ge(a_full, ring_a.take())
            copy(wgu[:, 1, 0:INNER], ring_a.bank[:, 0:INNER]).then_inc(C.give(a_drained), 1)
            act.wait_ge(a_full, ring_a.take())
            o = ring_a.bank
            copy(wdq[:, 0:2, :], o[:, 0:256].rearrange("p (t c) -> p t c", t=2))
            copy(wdq[0:96, 2, :], o[0:96, 256:384])
            copy(headsel[:], o[0:16, 384:512]).then_inc(C.give(a_drained), 1)
            act.wait_ge(a_full, ring_a.take())
            copy(dscaleB[:], ring_a.bank[:, 0:128]).then_inc(C.give(a_drained), 1)
            act.activation(clipe[:], clips[:], ACT.Exp, scale=-1.0).then_inc(clip_exp, 1)
            settle()

            C.section = "A"
            with act.Fori(0, NGROUPS) as it:
                take_ctx(2)
                take_n()
                take_quads(TOK, b0q)
                u = 0
                for b in range(GROUP):
                    if b >= 2:
                        act.wait_ge(e_used, C.next(e_used))
                    for j in range(SUBS):
                        exps(CTX, TOK, b, j, u)
                        u += 1
                last_exps_done()
                act.wait_ge(a_full, ring_a.take())
                copy(aT[:], ring_a.bank[:]).then_inc(C.give(a_drained), 1)
                take_n()
                for b in range(GROUP):
                    act.wait_ge(a_full, ring_a.take())
                    copy(xvs[:, b, :], ring_a.bank[:, 0:NV + 2 * NGATE]).then_inc(C.give(a_drained), 1)
                act.drain().then_inc(C.give(xv_ready), 1)
                act.activation(gexp[:, :, :, :].rearrange("p b h e -> p b (h e)"), xvs[:, :, NV:NV + NGATE], ACT.Exp,
                               scale=-1.0).then_inc(C.give(sig_ready), 1)
                for t in range(4):
                    act.wait_ge(a_full, ring_a.take())
                    copy(qf[:, t, :], ring_a.bank[:], scale=float(SHD) ** -0.5).then_inc(C.give(a_drained), 1)
                n_units = 2 * GROUP
                for u in range(n_units + LAG_V + 1):
                    if u < n_units:
                        exps(TOK, TOK, u // 2, u % 2, u)
                        if u == n_units - 1:
                            last_exps_done()
                    v = u - LAG_T
                    if 0 <= v < n_units:
                        act.wait_ge(a_full, ring_a.take())
                        copy(eT[:, v % 4, :], ring_a.bank[:]).then_inc(C.give(a_drained), 1)
                    v = u - LAG_V
                    if 0 <= v < n_units and v % 2 == 1:
                        act.wait_ge(a_full, ring_a.take())
                        copy(av[:, v // 2, :], ring_a.bank[:]).then_inc(C.give(a_drained), 1)
                        act.drain().then_inc(C.give(av_dve), 1)
                        act.drain().then_inc(C.give(av_pool), 1)
                for t in range(3):
                    rows = min(128, NV - 128 * t)
                    act.wait_ge(a_full, ring_a.take())
                    copy(ysT[0:rows, t, :], ring_a.bank[0:rows, :]).then_inc(C.give(a_drained), 1)
                act.wait_ge(a_full, ring_a.take())
                copy(kf[:, 0, 0:GROUP * CTX], ring_a.bank[:, 0:GROUP * CTX], bias=b1k[:]).then_inc(C.give(a_drained), 1)
                take_n()
                act.wait_ge(a_full, ring_a.take())
                copy(qf[:, 0, :], ring_a.bank[:], bias=b1q[:]).then_inc(C.give(a_drained), 1)
                exp_p(sc)
                act.wait_ge(a_full, ring_a.take())
                copy(aT[:], ring_a.bank[:], bias=b1v[:]).then_inc(C.give(a_drained), 1)
                take_n(scale=attn_w[:])
                take_quads(TOK)
                causal_heads(TOK)
                take_n(scale=ffn_w[:])
                act.wait_ge(c_ready, C.next(c_ready))
                act.activation(clog[:], clog[:], ACT.Exp).then_inc(C.give(cexp_ready), 1)
                take_n()
                exp_p(sc)
                act.wait_ge(a_full, ring_a.take())
                copy(nT_all[:, bass.ds(it * GROUP * TOK, GROUP * TOK)], ring_a.bank[:]).then_inc(C.give(a_drained), 1)
                settle(max_ready, e_used, pmax_ready, c_ready)

            C.section = "B"
            act.wait_ge(sx_ready, 1)
            with act.Fori(0, NGROUPS // 2) as it:
                for r in range(2):
                    for t, (r0, m) in enumerate(ITILES):
                        act.wait_ge(a_full, ring_a.take())
                        act.activation(hid[0:m, t, :], ring_a.bank[0:m, :], ACT.Silu, scale=actscale[0:m, t:t + 1]).then_inc(C.give(a_drained), 1)
                        act.drain().then_inc(C.give(sil_ready), 1)
                settle()

            C.section = "C"
            with act.Fori(0, NGROUPS) as it:
                take_ctx(1)
                take_quads(CTX)
                take_n()
                causal_heads(CTX)
                take_n()
                for t in range(4):
                    act.wait_ge(a_full, ring_a.take())
                    act.activation(hid[:, t, :], ring_a.bank[:], ACT.Relu, bias=b31[:, t:t + 1]).then_inc(C.give(a_drained), 1)
                settle(max_ready)

        @block.vector
        def _(dve):
            dve.wait_ge(loaded, NLOAD)
            dve.wait_ge(consts, NCONST)
            ring_d, ring_s = Ring(D, d_full, d_drained), Ring(SC, s_full, s_drained)
            units = [0]

            def settle(*sems):
                dve.wait_ge(dve_step, C.last(dve_step))
                for s in (*sems, dve_step):
                    C.settle(dve, s)
                for ring in (ring_d, ring_s):
                    if ring.taken:
                        C.settle(dve, ring.full, ring.taken)
                ring_d.taken = ring_s.taken = units[0] = 0

            def softmax_scale(probs):
                reduce(z1[:], probs, ALU.add).then_inc(C.give(dve_step), 1)
                dve.wait_ge(dve_step, C.last(dve_step))
                dve.reciprocal(z1[:], z1[:]).then_inc(C.give(dve_step), 1)
                dve.wait_ge(dve_step, C.last(dve_step))
                tt(work[:], probs, z1[:].unsqueeze(2).broadcast_to([128, GROUP, CTX]), ALU.mult)\
                    .then_inc(C.give(p_ready), 1)

            tt, ts, stt = dve.tensor_tensor, dve.tensor_scalar, dve.scalar_tensor_tensor

            def reduce(dst, src, op, **kw):
                return dve.tensor_reduce(dst, src, X, op, **kw)

            def normalise(src, dst, centre=True, to_pe=True):
                for b in range(GROUP):
                    dve.bn_stats(stats[:, b, :], src[:, b, :]).then_inc(C.give(dve_step), 1)
                dve.wait_ge(dve_step, C.last(dve_step))
                for b in range(GROUP):
                    ins = dve.bn_aggr(mv[:, b, :], stats[:, b, :])
                    if centre and b == GROUP - 1:
                        ins.then_inc(C.give(var_ready), 1)
                    else:
                        ins.then_inc(C.give(dve_step), 1)
                if not centre:
                    dve.wait_ge(dve_step, C.last(dve_step))
                    tt(msq[:], mv[:, :, 0], mv[:, :, 0], ALU.mult).then_inc(C.give(dve_step), 1)
                    dve.wait_ge(dve_step, C.last(dve_step))
                    tt(mv[:, :, 1], mv[:, :, 1], msq[:], ALU.add).then_inc(C.give(var_ready), 1)
                dve.wait_ge(rstd_ready, C.next(rstd_ready))
                for b in range(GROUP):
                    if centre:
                        ins = ts(dst[:, b, :], src[:, b, :], mv[:, b, 0:1], rstd[:, b:b + 1], ALU.subtract, ALU.mult)
                    else:
                        ins = ts(dst[:, b, :], src[:, b, :], rstd[:, b:b + 1], None, ALU.mult)
                    if b < GROUP - 1:
                        ins.then_inc(C.give(dve_step), 1)
                if to_pe:
                    ins.then_inc(C.give(n_ready), 1)
                else:
                    ins.then_inc(C.give(dve_step), 1)
                    dve.wait_ge(dve_step, C.last(dve_step))

            def take_subs(cols, scale, bias=None):
                dve.wait_ge(d_full, ring_d.take())
                o = ring_d.bank
                for j in range(SUBS):
                    src = o[:, 0:GROUP * cols].rearrange("p (b t) -> p b t", b=GROUP)
                    dst = sub_rows[:, :, j, 0:cols]
                    if bias is None:
                        ins = ts(dst, src, scale[:, j:j + 1], None, ALU.mult)
                    else:
                        ins = ts(dst, src, bias[:], scale[:, j:j + 1], ALU.add, ALU.mult)
                ins.then_inc(C.give(d_drained), 1)

            def per_head(v, b=None):
                return v.rearrange("p (g j d) -> p g j d", g=QUADS, j=SUBS)

            def unit_max(rows, width, b, j):
                dve.wait_ge(s_full, ring_s.take())
                o = ring_s.bank[0:rows, 0:4 * width].rearrange("p (g t) -> p g t", g=4)
                reduce(negmax[0:rows, b, 4 * j:4 * j + 4], o, ALU.max, negate=True).then_inc(C.give(max_ready), 1)

            def unit_sum(rows, width, b, j, u):
                dve.wait_ge(e_before, C.at(e_before, units[0] + u + 2))
                reduce(zsum[0:rows, b, 4 * j:4 * j + 4],
                            e[0:rows, u % 8, 0:4 * width].rearrange("p (g t) -> p g t", g=4), ALU.add).then_inc(C.give(dve_step), 1)

            def units_done(k):
                units[0] += k + 1

            def add_to_x(bias=None):
                dve.wait_ge(d_full, ring_d.take())
                o = ring_d.bank
                tt(xg[:], o[:].rearrange("p (b c) -> p b c", b=GROUP), xg[:], ALU.add).then_inc(C.give(d_drained), 1)
                dve.drain()

            def bias_to_x(bias):
                dve.drain()
                tt(xg[:], xg[:], bias[:].unsqueeze(1).broadcast_to([128, GROUP, CH]), ALU.add).then_inc(C.give(dve_step), 1)
                dve.wait_ge(dve_step, C.last(dve_step))

            def causal_heads(keys):
                n_units = GROUP * SUBS
                for u in range(n_units + 2):
                    if u < n_units:
                        unit_max(TOK, keys, u // SUBS, u % SUBS)
                    v = u - 2
                    if v >= 0:
                        unit_sum(TOK, keys, v // SUBS, v % SUBS, v)
                units_done(n_units)
                dve.wait_ge(dve_step, C.last(dve_step))
                dve.reciprocal(rz[:], zsum[:]).then_inc(C.give(rz_ready), 1)
                dve.wait_ge(d_full, ring_d.take())
                o = ring_d.bank
                dve.wait_ge(rzB_ready, C.next(rzB_ready))
                tt(aT[:], o[:], rzB[:], ALU.mult).then_inc(C.give(d_drained), 1)

            def top2(mask, logits, rank, segs, n_):
                def view(t):
                    return t.rearrange("p (b s e) -> p b s e", b=GROUP, e=n_)

                size = GROUP * segs * n_
                first, t1, t2 = (view(tsel[:, i, 0:size]) for i in range(3))
                m = tm[:, 0, 0:GROUP * segs].rearrange("p (b s) -> p b s", b=GROUP)
                r = tm[:, 1, 0:GROUP * segs].rearrange("p (b s) -> p b s", b=GROUP)

                def wide(v):
                    return v.unsqueeze(3).broadcast_to([128, GROUP, segs, n_])
                src = logits
                for i in range(2):
                    reduce(m, src, ALU.max).then_inc(C.give(dve_step), 1)
                    dve.wait_ge(dve_step, C.last(dve_step))
                    tt(t1, src, wide(m), ALU.is_ge).then_inc(C.give(dve_step), 1)
                    dve.wait_ge(dve_step, C.last(dve_step))
                    tt(t1, t1, rank, ALU.mult).then_inc(C.give(dve_step), 1)
                    dve.wait_ge(dve_step, C.last(dve_step))
                    reduce(r, t1, ALU.max).then_inc(C.give(dve_step), 1)
                    dve.wait_ge(dve_step, C.last(dve_step))
                    tt(first if i == 0 else t1, t1, wide(r), ALU.is_equal).then_inc(C.give(dve_step), 1)
                    dve.wait_ge(dve_step, C.last(dve_step))
                    if i == 0:
                        ts(t2, first, -BIG, None, ALU.mult).then_inc(C.give(dve_step), 1)
                        dve.wait_ge(dve_step, C.last(dve_step))
                        tt(t2, t2, logits, ALU.add).then_inc(C.give(dve_step), 1)
                        dve.wait_ge(dve_step, C.last(dve_step))
                        src = t2
                tt(mask, first, t1, ALU.add).then_inc(C.give(dve_step), 1)
                dve.wait_ge(dve_step, C.last(dve_step))

            def quantise(dst, src, inverse, m, w):
                ts(w, src, inverse, ROUND, ALU.mult, ALU.add).then_inc(C.give(dve_step), 1)
                dve.wait_ge(dve_step, C.last(dve_step))
                ts(w, w, ROUND + QMAX, ROUND - QMAX - 1.0, ALU.min, ALU.max).then_inc(C.give(dve_step), 1)
                dve.wait_ge(dve_step, C.last(dve_step))
                return ts(dst, w, ROUND, None, ALU.subtract)

            C.section = "setup"
            dve.sem_inc(group_free, 1)
            dve.sem_inc(a_drained, 2)
            dve.sem_inc(d_drained, 2)
            dve.sem_inc(s_drained, 4)
            dve.sem_inc(prod_free, 2)
            dve.sem_inc(oprod_free, 1)
            dve.sem_inc(ctxin_free, 1)
            dve.sem_inc(n_read, 1)
            for w in range(2):
                for t, (r0, m) in enumerate(ITILES):
                    reduce(wscale[0:m, w, t:t + 1], wraw[0:m, w, t, :], ALU.max, apply_absolute_value=True).then_inc(C.give(dve_step), 1)
                    dve.wait_ge(dve_step, C.last(dve_step))
                    ts(wscale[0:m, w, t:t + 1], wscale[0:m, w, t:t + 1], 1.0 / QMAX, None, ALU.mult).then_inc(C.give(dve_step), 1)
                    dve.wait_ge(dve_step, C.last(dve_step))
                    dve.reciprocal(winv[0:m, w, t:t + 1], wscale[0:m, w, t:t + 1]).then_inc(C.give(dve_step), 1)
                    dve.wait_ge(dve_step, C.last(dve_step))
                    ins = quantise(wraw[0:m, w, t, :], wraw[0:m, w, t, :], winv[0:m, w, t:t + 1], m,
                                   wk32[0:m, 0, 0:128])
                    if t < 2:
                        ins.then_inc(C.give(dve_step), 1)
                        dve.wait_ge(dve_step, C.last(dve_step))
                ins.then_inc(C.give(w_ready), 1)
                dve.drain()
            reduce(dscale[:], wdraw[:], ALU.max, apply_absolute_value=True).then_inc(C.give(dve_step), 1)
            dve.wait_ge(dve_step, C.last(dve_step))
            ts(dscale[:], dscale[:], 1.0 / QMAX, None, ALU.mult).then_inc(C.give(dve_step), 1)
            dve.wait_ge(dve_step, C.last(dve_step))
            dve.reciprocal(winv[:, 0, 0:1], dscale[:]).then_inc(C.give(dve_step), 1)
            dve.wait_ge(dve_step, C.last(dve_step))
            quantise(wdraw[:], wdraw[:], winv[:, 0, 0:1], 128, wk32[:, 0, 0:INNER]).then_inc(C.give(w_ready), 1)
            dve.memset(dscaleB[:], 1.0).then_inc(C.give(dve_step), 1)
            dve.wait_ge(dve_step, C.last(dve_step))
            ts(dscaleB[:], dscaleB[:], dscale[:], None, ALU.mult).then_inc(C.give(w_ready), 1)
            settle()

            C.section = "A"
            with dve.Fori(0, NGROUPS) as it:
                dve.wait_ge(xg_taken, C.next(xg_taken))
                dve.wait_ge(n_read, C.next(n_read))
                normalise(xg, n)
                bias_to_x(b0o)
                take_subs(CTX, subscale, b0k)
                dve.wait_ge(d_full, ring_d.take())
                o = ring_d.bank
                tt(vg[0:CTX], o[0:CTX].rearrange("p (b c) -> p b c", b=GROUP),
                        b0v[0:CTX].unsqueeze(1).broadcast_to([CTX, GROUP, CH]), ALU.add).then_inc(C.give(d_drained), 1)
                dve.drain()
                n_units = GROUP * SUBS
                for u in range(n_units + 2):
                    if u < n_units:
                        unit_max(CTX, TOK, u // SUBS, u % SUBS)
                    v = u - 2
                    if v >= 0:
                        unit_sum(CTX, TOK, v // SUBS, v % SUBS, v)
                        if v % SUBS == SUBS - 1:
                            b = v // SUBS
                            dve.wait_ge(dve_step, C.last(dve_step))
                            dve.reciprocal(rz[0:CTX, b, :], zsum[0:CTX, b, :]).then_inc(C.give(dve_step), 1)
                            dve.wait_ge(dve_step, C.last(dve_step))
                            tt(vdiag[0:CTX, b].rearrange("p g (j c) -> p g j c", j=SUBS)[:, :, :, 0:HDIM],
                               per_head(vg[0:CTX, b, :]),
                               rz[0:CTX, b, :].rearrange("p (j g) -> p g j", j=SUBS).unsqueeze(3)
                               .broadcast_to([CTX, QUADS, SUBS, HDIM]), ALU.mult).then_inc(C.give(v_ready), 1)
                units_done(n_units)
                add_to_x()

                normalise(xg, n)
                for t in range(4):
                    dve.wait_ge(d_full, ring_d.take())
                    dve.tensor_copy(kf[:, t, :], ring_d.bank[:]).then_inc(C.give(d_drained), 1)
                dve.wait_ge(xv_ready, C.next(xv_ready))
                top2(gates[:], xvs[:, :, NV:].rearrange("p b (s e) -> p b s e", e=SE),
                     rank5[:].rearrange("p (b s) e -> p b s e", b=GROUP), 2 * SH, SE)
                dve.wait_ge(sig_ready, C.next(sig_ready))
                ts(gexp[:], gexp[:], 1.0, None, ALU.add).then_inc(C.give(dve_step), 1)
                dve.wait_ge(dve_step, C.last(dve_step))
                dve.reciprocal(gexp[:], gexp[:]).then_inc(C.give(dve_step), 1)
                dve.wait_ge(dve_step, C.last(dve_step))
                tt(gates[:, :, 0:SH, :], gates[:, :, 0:SH, :], gexp[:], ALU.mult).then_inc(C.give(gate_ready), 1)
                n_units = 2 * GROUP
                for u in range(n_units + LAG_V + 1):
                    if u < n_units:
                        unit_max(TOK, TOK, u // 2, u % 2)
                    v = u - 2
                    if 0 <= v < n_units:
                        unit_sum(TOK, TOK, v // 2, v % 2, v)
                        if v % 2 == 1:
                            b = v // 2
                            dve.wait_ge(dve_step, C.last(dve_step))
                            dve.reciprocal(rz[:, b, 0:SH], zsum[:, b, 0:SH]).then_inc(C.give(dve_step), 1)
                            dve.wait_ge(dve_step, C.last(dve_step))
                            og = gates[:, b, SH:, :].rearrange("p (t q) e -> p t q e", q=2)
                            tt(og, og, rz[:, b, 0:SH].rearrange("p (q t) -> p t q", q=2).unsqueeze(3)
                               .broadcast_to([128, 4, 2, SE]), ALU.mult).then_inc(C.give(ogate_ready), 1)
                    if u % 2 == 1 and u // 2 < GROUP:
                        b = u // 2
                        dve.wait_ge(prod_ready, C.next(prod_ready))
                        for ex in range(1, SE):
                            dve.wait_ge(prod_ready, C.next(prod_ready))
                            m = b * (SE - 1) + ex - 1
                            tt(vs[:, b, :], vs[:, b, :], prod[:, m % 2, :], ALU.add).then_inc(C.give(prod_free), 1)
                            dve.drain()
                        dve.drain().then_inc(C.give(v_ready), 1)
                for b in range(GROUP):
                    dve.wait_ge(av_dve, C.next(av_dve))
                    if b > 0:
                        dve.drain()
                    for ex in range(POOL_OUT, SE):
                        tt(oprod[:, ex, :].rearrange("p (h k) -> p h k", h=SH),
                                av[:, b, :].rearrange("p (h k) -> p h k", h=SH),
                                gates[:, b, SH:, ex].unsqueeze(2).broadcast_to([128, SH, SHD]), ALU.mult).then_inc(C.give(dve_step), 1)
                    dve.wait_ge(oprod_ready, C.next(oprod_ready))
                    dve.wait_ge(dve_step, C.last(dve_step))
                    reduce(ys[:, b, :].rearrange("p (e k) -> p e k", e=SE),
                           oprod[:].rearrange("p e (h k) -> p e k h", h=SH), ALU.add).then_inc(C.give(oprod_free), 1)
                dve.drain().then_inc(C.give(y_ready), 1)
                units_done(n_units)
                add_to_x()

                normalise(xg, n)
                bias_to_x(b1o)
                dve.wait_ge(d_full, ring_d.take())
                dve.tensor_copy(vg[0:CTX], ring_d.bank[0:CTX].rearrange("p (b c) -> p b c", b=GROUP)).then_inc(C.give(d_drained), 1)
                dve.wait_ge(d_full, ring_d.take())
                ts(sc[:], ring_d.bank[:, 0:GROUP * CTX].rearrange("p (b s) -> p b s", b=GROUP),
                        float(CH) ** -0.5, None, ALU.mult).then_inc(C.give(d_drained), 1)
                dve.drain()
                for r in range(TOPK // 8):
                    src = sc if r == 0 else work
                    for b in range(GROUP):
                        dve.max(top8[:, b, r, :], src[:, b, :]).then_inc(C.give(dve_step), 1)
                    dve.wait_ge(dve_step, C.last(dve_step))
                    if r == 0:
                        ts(negmax[:, :, 0], top8[:, :, 0, 0], -1.0, None, ALU.mult).then_inc(C.give(pmax_ready), 1)
                    for b in range(GROUP):
                        dve.match_replace(work[:, b, :], top8[:, b, r, :], src[:, b, :], -BIG).then_inc(C.give(dve_step), 1)
                    dve.wait_ge(dve_step, C.last(dve_step))
                dve.wait_ge(pexp_ready, C.next(pexp_ready))
                for b in range(GROUP):
                    stt(out=work[:, b, :], in0=work[:, b, :], scalar=-BIG, in1=e[:, 0, b * CTX:(b + 1) * CTX],
                             op0=ALU.is_equal, op1=ALU.mult).then_inc(C.give(dve_step), 1)
                dve.wait_ge(dve_step, C.last(dve_step))
                softmax_scale(work[:])
                add_to_x()

                normalise(xg, hres, to_pe=False)
                normalise(hres, n, centre=False)
                take_subs(TOK, subscale)
                dve.wait_ge(d_full, ring_d.take())
                o = ring_d.bank
                for j in range(SUBS):
                    ins = dve.tensor_copy(vdiag[:, :, :, 40 * j:40 * j + HDIM],
                                          o[:, 0:GROUP * 32].rearrange("p (b g d) -> p b g d", b=GROUP, g=QUADS))
                ins.then_inc(C.give(d_drained), 1)
                causal_heads(TOK)
                dve.wait_ge(d_full, ring_d.take())
                tt(hres[:], ring_d.bank[:].rearrange("p (b c) -> p b c", b=GROUP), hres[:], ALU.add).then_inc(C.give(d_drained), 1)
                dve.drain()
                normalise(hres, n, centre=False)
                tt(xg[:], xg[:], hres[:], ALU.add).then_inc(C.give(dve_step), 1)
                dve.wait_ge(d_full, ring_d.take())
                dve.tensor_copy(clog[:], ring_d.bank[:, 0:GROUP * ME].rearrange("p (b e) -> p b e", b=GROUP)).then_inc(C.give(d_drained), 1)
                dve.drain()
                c4 = clog[:].unsqueeze(2)
                top2(comb[:].unsqueeze(2), c4, rank8[:].unsqueeze(2), 1, ME)
                reduce(z1[:], clog[:], ALU.max).then_inc(C.give(dve_step), 1)
                dve.wait_ge(dve_step, C.last(dve_step))
                tt(clog[:], clog[:], z1[:].unsqueeze(2).broadcast_to([128, GROUP, ME]),
                   ALU.subtract).then_inc(C.give(c_ready), 1)
                dve.wait_ge(cexp_ready, C.next(cexp_ready))
                tt(comb[:], comb[:], clog[:], ALU.mult).then_inc(C.give(dve_step), 1)
                dve.wait_ge(dve_step, C.last(dve_step))
                reduce(z1[:], comb[:], ALU.add).then_inc(C.give(dve_step), 1)
                dve.wait_ge(dve_step, C.last(dve_step))
                dve.reciprocal(z1[:], z1[:]).then_inc(C.give(dve_step), 1)
                dve.wait_ge(dve_step, C.last(dve_step))
                tt(comb[:], comb[:], z1[:].unsqueeze(2).broadcast_to([128, GROUP, ME]), ALU.mult).then_inc(C.give(dve_step), 1)
                dve.wait_ge(dve_step, C.last(dve_step))
                for b in range(GROUP):
                    for half in range(2):
                        dve.wait_ge(d_full, ring_d.take())
                        o = ring_d.bank
                        for ex in range(4):
                            w = 4 * half + ex
                            ins = stt(out=xg[:, b, :], in0=o[:, ex * 128:(ex + 1) * 128], scalar=comb[:, b, w:w + 1],
                                      in1=xg[:, b, :], op0=ALU.mult, op1=ALU.add)
                            if ex < 3:
                                ins.then_inc(C.give(dve_step), 1)
                                dve.wait_ge(dve_step, C.last(dve_step))
                        ins.then_inc(C.give(d_drained), 1)
                        dve.drain()

                normalise(xg, n)
                dve.wait_ge(d_full, ring_d.take())
                dve.tensor_copy(sc[:], ring_d.bank[:, 0:GROUP * CTX].rearrange("p (b s) -> p b s", b=GROUP)).then_inc(C.give(d_drained), 1)
                dve.drain()
                reduce(negmax[:, :, 0], sc[:], ALU.max, negate=True).then_inc(C.give(pmax_ready), 1)
                dve.wait_ge(pexp_ready, C.next(pexp_ready))
                softmax_scale(e[:, 0, 0:GROUP * CTX].rearrange("p (b s) -> p b s", b=GROUP))
                add_to_x()
                normalise(xg, n)
                dve.drain()
                reduce(amax[:, bass.ds(it, 1)], n[:].rearrange("p b c -> p (b c)"), ALU.max, apply_absolute_value=True)
                dve.tensor_copy(x_all[:, bass.ds(it * GROUP, GROUP), :], xg[:]).then_inc(group_free, 1)
                settle(n_read, xg_taken, rstd_ready, e_before, xv_ready, sig_ready, prod_ready, av_dve, oprod_ready,
                       pexp_ready, rzB_ready, cexp_ready)

            def act_scale(i):
                s = actscale[:, 6 + i:7 + i]
                tt(s, gmax[:, 2 * i + 1:2 * i + 2], sigm[:, i:i + 1], ALU.mult).then_inc(C.give(dve_step), 1)
                dve.wait_ge(dve_step, C.last(dve_step))
                ts(s, s, 1.0 / QMAX, None, ALU.mult).then_inc(C.give(dve_step), 1)
                dve.wait_ge(dve_step, C.last(dve_step))
                dve.reciprocal(ainv[:, i:i + 1], s).then_inc(C.give(dve_step), 1)
                dve.wait_ge(dve_step, C.last(dve_step))

            C.section = "AB"
            dve.drain()
            reduce(gmax[:, 0:1], amax[:], ALU.max).then_inc(amax_ready, 1)
            dve.wait_ge(clip_exp, 1)
            ts(sigm[:], clipe[:], 1.0, None, ALU.add).then_inc(C.give(dve_step), 1)
            dve.wait_ge(dve_step, C.last(dve_step))
            dve.reciprocal(sigm[:], sigm[:]).then_inc(C.give(dve_step), 1)
            dve.wait_ge(dve_step, C.last(dve_step))
            dve.wait_ge(gmax_ready, 1)
            act_scale(0)
            for t, (r0, m) in enumerate(ITILES):
                ts(upscale[0:m, t:t + 1], wscale[0:m, 1, t:t + 1], actscale[0:m, 6:7], None, ALU.mult).then_inc(C.give(dve_step), 1)
                ins = ts(actscale[0:m, t:t + 1], wscale[0:m, 0, t:t + 1], actscale[0:m, 6:7], None, ALU.mult)
            ins.then_inc(sx_ready, 1)
            settle()

            C.section = "B"
            with dve.Fori(0, NGROUPS // 2) as it:
                def activations(r):
                    cols = bass.ds((it * 2 + r) * GROUP * TOK, GROUP * TOK)
                    quantise(xq[:, r, :], nT_all[:, cols], ainv[:, 0:1], 128, wk32[:, r, :]).then_inc(C.give(q_ready), 1)
                dve.drain()
                for r in range(2):
                    activations(r)
                for r in range(2):
                    cols = bass.ds((it * 2 + r) * GROUP * TOK, GROUP * TOK)
                    for t, (r0, m) in enumerate(ITILES):
                        dve.wait_ge(d_full, ring_d.take())
                        o = ring_d.bank
                        dve.wait_ge(sil_ready, C.next(sil_ready))
                        stt(out=wk32[0:m, 2 + t % 2, :], in0=o[0:m, :], scalar=upscale[0:m, t:t + 1],
                                 in1=hid[0:m, t, :], op0=ALU.mult, op1=ALU.mult).then_inc(C.give(d_drained), 1)
                        dve.drain()
                        dve.tensor_copy(h_all[0:m, t, cols], wk32[0:m, 2 + t % 2, :]).then_inc(C.give(dve_step), 1)
                        reduce(hmax[0:m, bass.ds((it * 2 + r) * 3 + t, 1)], wk32[0:m, 2 + t % 2, :], ALU.max,
                                    apply_absolute_value=True).then_inc(C.give(dve_step), 1)
                        dve.wait_ge(dve_step, C.last(dve_step))
                settle(sil_ready)

            C.section = "BC"
            dve.drain()
            reduce(gmax[:, 2:3], hmax[:], ALU.max).then_inc(amax_ready, 1)
            dve.wait_ge(gmax_ready, 2)
            act_scale(1)
            ts(dscaleB[:], dscaleB[:], actscale[:, 7:8], None, ALU.mult).then_inc(C.give(dve_step), 1)
            settle()

            C.section = "C"
            with dve.Fori(0, NGROUPS) as it:
                for t, (r0, m) in enumerate(ITILES):
                    ins = quantise(hq[0:m, t, :], h_all[0:m, t, bass.ds(it * GROUP * TOK, GROUP * TOK)],
                                   ainv[0:m, 1:2], m, wk32[0:m, t, :])
                    if t < 2:
                        ins.then_inc(C.give(dve_step), 1)
                ins.then_inc(C.give(q_ready), 1)
                dve.wait_ge(xg_taken, C.next(xg_taken))
                dve.wait_ge(d_full, ring_d.take())
                o = ring_d.bank
                tt(hres[:], o[:].rearrange("p (b c) -> p b c", b=GROUP),
                        dscaleB[:].unsqueeze(1).broadcast_to([128, GROUP, CH]), ALU.mult).then_inc(C.give(d_drained), 1)
                dve.drain()
                tt(xg[:], xg[:], hres[:], ALU.add).then_inc(C.give(dve_step), 1)
                dve.wait_ge(dve_step, C.last(dve_step))
                normalise(xg, n)
                dve.wait_ge(d_full, ring_d.take())
                o = ring_d.bank
                for j in range(SUBS):
                    ins = dve.tensor_copy(vdiag[0:CTX, :, :, 40 * j:40 * j + HDIM],
                                          o[0:CTX].rearrange("p (b g j d) -> p b g j d", b=GROUP, g=QUADS,
                                                             j=SUBS)[:, :, :, j, :])
                ins.then_inc(C.give(d_drained), 1)
                take_subs(TOK, subscale)
                causal_heads(CTX)
                add_to_x()
                normalise(xg, n)
                bias_to_x(b32)
                dve.wait_ge(d_full, ring_d.take())
                tt(x_all[:, bass.ds(it * GROUP, GROUP), :], ring_d.bank[:].rearrange("p (b c) -> p b c", b=GROUP),
                        xg[:], ALU.add).then_inc(C.give(d_drained), 1)
                dve.drain().then_inc(C.give(x_done), 1)
                dve.drain().then_inc(group_free, 1)
                settle(xg_taken, rstd_ready, e_before, rzB_ready)
            C.given["A", group_free.name] = C.given["C", group_free.name] = 1

        C.check()
    return nc


def kernel(**inputs):
    import numpy as np
    import concourse.bacc as bacc
    from concourse.bass_utils import run_bass_kernel_spmd

    nc = bacc.Bacc("TRN2", target_bir_lowering=False, num_devices=1)
    turned = {"L1_xattn_Wq", "L1_xattn_Wk", "L1_xattn_Wv", "L1_xattn_Wo", "L1_ffn_wq", "L1_ffn_wk", "L1_ffn_wv",
              "L1_ffn_wo", "L1_ffn_gate_w", "L3_xattn_Wq", "L3_xattn_Wk", "L3_xattn_Wv", "L3_xattn_Wo"}
    arrays, d = {}, {}
    for name, value in inputs.items():
        a = np.asarray(value)
        if name in turned:
            a = a.T
        if name == "L1_ffn_expert_w":
            a = a.transpose(0, 2, 1)
        a = np.ascontiguousarray(a)
        arrays["in_" + name] = a
        d[name] = nc.dram_tensor("in_" + name, a.shape, mybir.dt.from_np(a.dtype), kind="ExternalInput").ap()
    out = nc.dram_tensor("out", (BATCH, TOK, CH), FP32, kind="ExternalOutput").ap()
    four_layers(nc, d, out)
    r = run_bass_kernel_spmd(nc, [arrays], core_ids=[0])
    return r.results[0]["out"]
```

```python
import concourse.bass as bass
from concourse import mybir
from contextlib import ExitStack

FP32 = mybir.dt.float32
BF16 = mybir.dt.bfloat16
ACT = mybir.ActivationFunctionType
ALU = mybir.AluOpType
X = mybir.AxisListType.X

BATCH, TOK, CH, CTX = 32, 128, 128, 77
SEQS = 4
NGROUPS = BATCH // SEQS
HEADS, HDIM = 16, 8
QUADS, SUBS = 4, 4
SH, SHD, SE = 8, 64, 5
ME = 8
INNER = 352
ITILES = [(0, 128), (128, 128), (256, 96)]
WIDTH = 512
TOPK = 32
BIG = 1.0e30
ROUND = 12582912.0
QMAX = 127.0
LN_EPS, RMS_EPS = 1e-5, 1e-6
LAG_T, LAG_V = 2, 3
POOL_OUT = 2
NCONST = 15
ORDER = {
    ("first", "tensor"):
        "pppppppppqppppppppqppppppppqpppppppqppppppppppppppppppppppppppppppppppppppppppp",
    ("first", "scalar"):
        "pppppppqppppqppppqppppqpppppppppppppppppppppppppppppppppppp",
    ("first", "vector"):
        "ppppppqqpppqqpqqppqppqqpppppppppppppppppppppppppppppppppppppppppppp",
    ("A", "gpsimd"):
        "qpqqpppppppppppppqpppppppppppppqq",
    ("A", "tensor"):
        "qppqpqqppqpqqppqpqpppqqqppqqqppqpqqqqqppppqpqpqpqpqqqqqpppppqqpppqqqqpppppqqqqqqqqqppqqp"
        "qpqqpqpqqqqpqqpqppqqqqppqpppppqpppppqqqqpppppqqpppppqpqpqqpqpqpqqq",
    ("A", "scalar"):
        "qpqpqqpqqpppqpqpqqpqqqqppqqqppqpqqpqqqppqppqqqpqqqqqpqpqpqpqpqqqqqppqppqppqpppppppqpppqp"
        "ppppppppppppqpqqq",
    ("A", "vector"):
        "qqppqqppqqqqqqppqqqppqqqppqpqqqpqqppqpqpppqpqpqppppqpqppqqpqqqppppppppqpppppqpppqqpqpppq"
        "qqqqqqppppqqqpppqppqqqqqqqpqqq",
    ("B", "tensor"):
        "qpqpqp",
    ("B", "scalar"):
        "qpqpqp",
    ("B", "vector"):
        "qpqpqqpp",
    ("C", "gpsimd"):
        "pqpq",
    ("C", "tensor"):
        "ppqqpqpqpqpqpqpqpqpqpqpqpqpqpqpqpqpqpqpqpqpqpqpqpqpqpqpqpqpqpqpqpqpqpqpqpqpqpqqppqpqqppq"
        "pqpqpqppqqpqppqqpqppqqppqqpqpqppqqpqpqpqqpqp",
    ("C", "scalar"):
        "ppqqpqpqpqpqpqqppqpqpqpqpqpqpqpqpqpqpqpqpqpqpqpqpqpqpqqppqqppqpppqqqppqqpqpqpqpqpqpq",
    ("C", "vector"):
        "pqpqpqppqqpqpqpqppqqppqqppqqppqqppqqppqqppqqppqqpqqppqqppqqpqqppqqpppppqqqpqpqppqqpqpqqp"
        "qp",
}
L0X_SCORES = [(u + 2 * (u // SUBS), "scores", u) for u in range(SEQS * SUBS)]
L0X_STEPS = sorted(L0X_SCORES + [(5.5 + u % SUBS + 6 * (u // SUBS), "heads", u) for u in range(SEQS * SUBS)])
L0X_STEPS_DVE = sorted(L0X_SCORES + [(6 * b + SUBS, "sums", SUBS * b) for b in range(SEQS)])


class Counts:

    def __init__(self):
        self.section, self.given, self.waited, self.seen = None, {}, {}, {}

    def give(self, sem):
        key = self.section, sem.name
        self.given[key] = self.given.get(key, 0) + 1
        return sem

    def at(self, sem, n):
        key = self.section, sem.name
        self.waited[key] = max(self.waited.get(key, 0), n)
        return n

    def next(self, sem):
        key = self.section, sem.name
        self.seen[key] = self.seen.get(key, 0) + 1
        return self.at(sem, self.seen[key])

    def last(self, sem):
        return self.at(sem, self.given[self.section, sem.name])

    def settle(self, eng, sem, n=None):
        key = self.section, sem.name
        n = self.waited[key] if n is None else n
        self.waited[key] = n
        eng.sem_inc(sem, -n)

    def check(self):
        assert self.given == self.waited, {k: (self.given.get(k), self.waited.get(k))
                                           for k in {*self.given, *self.waited}
                                           if self.given.get(k) != self.waited.get(k)}


def in_order(order, p_stages, q_stages):
    stages = {"p": p_stages, "q": q_stages}
    for each in stages.values():
        next(each)
    for name in order:
        next(stages[name], None)
    assert all(next(each, "done") == "done" for each in stages.values())


def alone(stages):
    for _ in stages:
        pass


class Ring:

    def __init__(self, banks, full, drained):
        self.banks, self.full, self.drained, self.taken, self.bank = banks, full, drained, 0, None

    def take(self):
        self.bank = self.banks[self.taken % len(self.banks)]
        self.taken += 1
        return self.taken

    def item(self):
        return self.taken + len(self.banks)


def four_layers(nc, d, out):
    ctx = ExitStack()
    with ctx:
        def sb(name, shape, dt=FP32):
            return ctx.enter_context(nc.sbuf_tensor(name, shape, dt))

        def sem(name):
            return ctx.enter_context(nc.semaphore(name))

        ident = sb("ident", [128, 128])
        identb = sb("identb", [128, 128], BF16)
        causal = sb("causal", [128, 4, 128], BF16)
        diag = sb("diag", [128, SUBS, QUADS])
        subone = sb("subone", [128, SUBS])
        subscale = sb("subscale", [128, SUBS])
        headsel = sb("headsel", [16, 128])
        rank5 = sb("rank5", [128, SEQS * 2 * SH, SE])
        rank8 = sb("rank8", [128, SEQS, ME])
        minushalf = sb("minushalf", [128, SEQS])

        w0q, w0k, w0v, w0o = (sb(f"w0{n}", [128, 128]) for n in "qkvo")
        b0q, b0k = (sb(f"b0{n}", [128, 1]) for n in "qk")
        b0v, b0o = (sb(f"b0{n}", [128, 128]) for n in "vo")
        wsq, wsk = (sb(f"ws{n}", [128, SH * SHD]) for n in "qk")
        NV, NGATE = SE * SHD, SH * SE
        wsv = sb("wsv", [128, NV + 2 * NGATE])
        wso = sb("wso", [128, 3, 128])
        w1q, w1k, w1v, w1o = (sb(f"w1{n}", [128, 128]) for n in "qkvo")
        b1q, b1k, b1v = (sb(f"b1{n}", [128, 1]) for n in "qkv")
        b1o = sb("b1o", [128, 128])
        wgq, wgk, wgv, wgo = (sb(f"wg{n}", [128, m]) for n, m in (("q", 128), ("k", 128), ("v", 32), ("o", 128)))
        attn_w, ffn_w = sb("attn_w", [128, 1]), sb("ffn_w", [128, 1])
        wgate = sb("wgate", [128, ME])
        wexp = sb("wexp", [128, ME * 128])
        w3q, w3k, w3v, w3o = (sb(f"w3{n}", [128, 128]) for n in "qkvo")
        w31 = sb("w31", [128, WIDTH])
        b31 = sb("b31", [128, 4])
        w32 = sb("w32", [128, 4, 128])
        b32 = sb("b32", [128, 128])
        clips = sb("clips", [128, 2])
        wgu = sb("wgu", [128, 2, 3 * 128], BF16)
        wdq = sb("wdq", [128, 3, 128], BF16)
        wscale = sb("wscale", [128, 2, 3])
        dscale = sb("dscale", [128, 1])
        dscaleB = sb("dscaleB", [128, 128])
        actscale = sb("actscale", [128, 8])
        ainv = sb("ainv", [128, 2])
        upscale = sb("upscale", [128, 3])
        winv = sb("winv", [128, 2, 3])
        clipe = sb("clipe", [128, 2])
        sigm = sb("sigm", [128, 2])

        nT_all = sb("nT_all", [128, BATCH * TOK])
        h_all = sb("h_all", [128, 3, BATCH * TOK])
        amax = sb("amax", [128, NGROUPS])
        hmax = sb("hmax", [128, 3 * NGROUPS])
        gmax = sb("gmax", [128, 4])
        hf = h_all[:, :, :].rearrange("p a b -> p (a b)")
        at = [0]

        def part(size):
            at[0] += size
            return hf[:, at[0] - size:at[0]]
        oprod = part(SE * 512).rearrange("p (e n) -> p e n", e=SE)
        oprod_ready, oprod_free = sem("oprod_ready"), sem("oprod_free")
        banks = [ctx.enter_context(nc.psum_tensor(f"bank{i}", [128, 512], FP32)) for i in range(8)]

        class Stream:

            def __init__(self, i):
                def sbi(name, shape, dt=FP32):
                    return sb(f"{name}_{i}", shape, dt)

                self.index = i
                self.xg = sbi("xg", [128, SEQS, CH])
                self.ctxg = sbi("ctxg", [CTX, SEQS, CH])
                self.ctxT = sbi("ctxT", [128, SEQS, CTX])
                self.ctxT2 = self.ctxT[:, :, :].rearrange("p b s -> p (b s)")
                self.n = sbi("n", [128, SEQS, CH])
                self.nT = sbi("nT", [128, SEQS * TOK])
                self.stats = sbi("stats", [128, SEQS, 6])
                self.mv = sbi("mv", [128, SEQS, 2])
                self.rstd = sbi("rstd", [128, SEQS])
                self.quad_rows = sbi("quad_rows", [128, SEQS, QUADS, 128])
                self.sub_rows = sbi("sub_rows", [128, SEQS, SUBS, 128])
                self.vdiag = sbi("vdiag", [128, SEQS, QUADS, 160])
                self.e = sbi("e", [128, 4, 512])
                self.eT = sbi("eT", [128, 2, 512])
                self.negmax = sbi("negmax", [128, SEQS, 16])
                self.zsum = sbi("zsum", [128, SEQS, 16])
                self.rz = sbi("rz", [128, SEQS, 16])
                self.aT = sbi("aT", [128, SEQS * TOK])
                self.hq = sbi("hq", [128, 3, SEQS * TOK], BF16)
                self.xq = self.hq[:, 0, :]
                self.kf = self.sub_rows[:, :, :, :].rearrange("p b j n -> p b (j n)")
                self.rzT = self.n[:, :, :].rearrange("p b c -> p (b c)")[0:16, :]
                self.rzB = self.nT
                self.vg = self.aT[:, :].rearrange("p (b c) -> p b c", b=SEQS)
                self.hid = self.e
                self.wk32 = self.e[:, 1:4, :]

                self.a_full, self.a_drained = sem(f"a_full_{i}"), sem(f"a_drained_{i}")
                self.d_full, self.d_drained = sem(f"d_full_{i}"), sem(f"d_drained_{i}")
                self.s_full, self.s_drained = sem(f"s_full_{i}"), sem(f"s_drained_{i}")
                bank_a, bank_d, banks_s = banks[i:i + 1], banks[2 + i:3 + i], banks[4 + 2 * i:6 + 2 * i]
                self.pe_a = Ring(bank_a, self.a_full, self.a_drained)
                self.act_a = Ring(bank_a, self.a_full, self.a_drained)
                self.pe_d = Ring(bank_d, self.d_full, self.d_drained)
                self.dve_d = Ring(bank_d, self.d_full, self.d_drained)
                self.pe_s = Ring(banks_s, self.s_full, self.s_drained)
                self.act_s = Ring(banks_s, self.s_full, self.s_drained)
                self.dve_s = Ring(banks_s, self.s_full, self.s_drained)

                self.x_in, self.ctx_in = sem(f"x_in_{i}"), sem(f"ctx_in_{i}")
                self.x_done, self.x_stored = sem(f"x_done_{i}"), sem(f"x_stored_{i}")
                self.var_ready, self.rstd_ready = sem(f"var_ready_{i}"), sem(f"rstd_ready_{i}")
                self.n_ready = sem(f"n_ready_{i}")
                self.max_ready, self.sums_ready = sem(f"max_ready_{i}"), sem(f"sums_ready_{i}")
                self.e_ready = sem(f"e_ready_{i}")
                self.rz_ready, self.rzB_ready = sem(f"rz_ready_{i}"), sem(f"rzB_ready_{i}")
                self.q_ready, self.sil_ready = sem(f"q_ready_{i}"), sem(f"sil_ready_{i}")

        class StreamP(Stream):

            def __init__(self, i):
                super().__init__(i)
                self.tm = sb("tm_p", [128, 2, SEQS * 2 * SH])
                self.gates = sb("gates", [128, SEQS, 2 * SH, SE])
                self.gexp = sb("gexp", [128, SEQS, SH, SE])
                self.qf = part(4 * SEQS * TOK).rearrange("p (t n) -> p t n", t=4)
                self.xvs = part(SEQS * 400).rearrange("p (b n) -> p b n", b=SEQS)
                self.vs = part(SEQS * 512).rearrange("p (b n) -> p b n", b=SEQS)
                self.prod = part(512)
                self.av = part(2 * 512).rearrange("p (b n) -> p b n", b=2)
                self.ys = part(SEQS * SE * SHD).rearrange("p (b n) -> p b n", b=SEQS)
                self.tsel = self.eT[:, :, :].rearrange("p r n -> p (r n)")
                self.ysT = self.qf[:, 0:3, :]
                self.v_ready, self.e_used, self.v_gated = sem("v_ready"), sem("e_used"), sem("v_gated")
                self.xv_ready, self.sig_ready = sem("xv_ready"), sem("sig_ready")
                self.gate_ready, self.ogate_ready = sem("gate_ready"), sem("ogate_ready")
                self.av_dve, self.av_pool = sem("av_dve"), sem("av_pool")
                self.y_ready = sem("y_ready")

        class StreamQ(Stream):

            def __init__(self, i):
                super().__init__(i)
                self.msq = sb("msq", [128, SEQS])
                self.tm = sb("tm_q", [128, 2, SEQS])
                self.q1 = part(SEQS * TOK)
                self.top8 = sb("top8", [128, SEQS, 4, 8])
                self.work = part(SEQS * CTX).rearrange("p (b s) -> p b s", b=SEQS)
                self.sc = part(SEQS * CTX).rearrange("p (b s) -> p b s", b=SEQS)
                self.z1 = sb("z1", [128, SEQS])
                self.hres = sb("hres", [128, SEQS, CH])
                self.comb = sb("comb", [128, SEQS, ME])
                self.clog = sb("clog", [128, SEQS, ME])
                self.tsel = sb("tsel_q", [128, 3 * SEQS * ME])
                self.n_read = sem("n_read")
                self.pmax_ready, self.pexp_ready = sem("pmax_ready"), sem("pexp_ready")
                self.p_ready = sem("p_ready")
                self.c_ready, self.cexp_ready = sem("c_ready"), sem("cexp_ready")

        p, q = streams = StreamP(0), StreamQ(1)
        assert at[0] <= 3 * BATCH * TOK

        wraw = q.kf[:, 0:2, 0:3 * 128].rearrange("p w (t c) -> p w t c", t=3)
        wdraw = q.kf[:, 2, 0:INNER]

        loaded_p, loaded_q = sem("loaded_p"), sem("loaded_q")
        consts, zeroed = sem("consts"), sem("zeroed")
        handed, p_free = sem("handed"), sem("p_free")
        x_ready, x_safe = sem("x_ready"), sem("x_safe")
        dve_step, pool_step = sem("dve_step"), sem("pool_step")
        w_ready, clip_exp = sem("w_ready"), sem("clip_exp")
        amax_ready, gmax_ready, sx_ready = sem("amax_ready"), sem("gmax_ready"), sem("sx_ready")

        C = Counts()
        ctx.enter_context(nc.allow_non_contiguous_dma(reason="a bias of 512 as columns, once"))
        block = ctx.enter_context(nc.Block())
        LOADS = []

        def load_weight(dst, src):
            LOADS.append((dst, src))
        col = lambda v: v.rearrange("(p a) -> p a", a=1)
        row = lambda v: v.rearrange("(a p) -> a p", a=1).broadcast_to([128, v.shape[0]])
        for dst, name in ((w0q, "Wq"), (w0k, "Wk"), (w0v, "Wv"), (w0o, "Wo")):
            load_weight(dst[:], d["L0_xattn_" + name])
        load_weight(b0q[:], col(d["L0_xattn_bq"]))
        load_weight(b0k[:], col(d["L0_xattn_bk"]))
        load_weight(b0v[:], row(d["L0_xattn_bv"]))
        load_weight(b0o[:], row(d["L0_xattn_bo"]))
        load_weight(wsq[:], d["L0_ffn_Wq"])
        load_weight(wsk[:], d["L0_ffn_Wk"])
        load_weight(wsv[:, 0:NV].rearrange("p (e k) -> p e k", e=SE), d["L0_ffn_Wv"].rearrange("e d k -> d e k"))
        load_weight(wsv[:, NV:NV + NGATE], d["L0_ffn_Ws"])
        load_weight(wsv[:, NV + NGATE:], d["L0_ffn_Wd"])
        wo = d["L0_ffn_Wo"].rearrange("e k c -> (e k) c")
        load_weight(wso[:, 0:2, :], wo[0:256].rearrange("(t p) c -> p t c", p=128))
        load_weight(wso[0:64, 2, :], wo[256:320])
        LOADS_P = len(LOADS)
        for dst, name in ((w1q, "Wq"), (w1k, "Wk"), (w1v, "Wv"), (w1o, "Wo")):
            load_weight(dst[:], d["L1_xattn_" + name])
        for dst, name in ((b1q, "bq"), (b1k, "bk"), (b1v, "bv")):
            load_weight(dst[:], col(d["L1_xattn_" + name]))
        load_weight(b1o[:], row(d["L1_xattn_bo"]))
        load_weight(wgq[:], d["L1_ffn_wq"])
        for j in range(SUBS):
            load_weight(wgk[:, :].rearrange("p (g j d) -> p g j d", g=QUADS, j=SUBS)[:, :, j, :],
                 d["L1_ffn_wk"].rearrange("c (g d) -> c g d", g=QUADS))
        load_weight(wgv[:], d["L1_ffn_wv"])
        load_weight(wgo[:], d["L1_ffn_wo"])
        load_weight(attn_w[:], col(d["L1_ffn_attn_norm_w"]))
        load_weight(ffn_w[:], col(d["L1_ffn_ffn_norm_w"]))
        load_weight(wgate[:], d["L1_ffn_gate_w"])
        load_weight(wexp[:, :].rearrange("p (e o) -> p e o", e=ME), d["L1_ffn_expert_w"].rearrange("e c o -> c e o"))
        for dst, name in ((w3q, "Wq"), (w3k, "Wk"), (w3v, "Wv"), (w3o, "Wo")):
            load_weight(dst[:], d["L3_xattn_" + name])
        load_weight(w31[:], d["L3_ffn_w1"])
        load_weight(b31[:], d["L3_ffn_b1"].rearrange("(t p) -> p t", p=128))
        load_weight(w32[:], d["L3_ffn_w2"].rearrange("(t p) c -> p t c", p=128))
        load_weight(b32[:], row(d["L3_ffn_b2"]))
        load_weight(clips[:, 0:1], d["L2_ffn_clip_x"].rearrange("(a p) -> a p", a=1).broadcast_to([128, 1]))
        load_weight(clips[:, 1:2], d["L2_ffn_clip_down"].rearrange("(a p) -> a p", a=1).broadcast_to([128, 1]))
        for w, name in ((0, "gate"), (1, "up")):
            for t, (r0, m) in enumerate(ITILES):
                load_weight(wraw[0:m, w, t, :], d["L2_ffn_w_" + name][r0:r0 + m])
        load_weight(wdraw[:], d["L2_ffn_w_down"])
        NLOAD_P, NLOAD_Q = 16 * LOADS_P, 16 * (len(LOADS) - LOADS_P)

        @block.sync
        def _(sp):
            def load(s, x, group):
                sp.dma_start(s.xg[:], x[bass.ds(group * SEQS, SEQS)].rearrange("b t c -> t b c")).then_inc(s.x_in, 16)
                sp.dma_start(s.ctxg[:], d["ctx_1024"][bass.ds(group * SEQS, SEQS)].rearrange("b t c -> t b c"))\
                    .then_inc(s.ctx_in, 16)

            def store(s, y, group):
                sp.dma_start(out[bass.ds(group * SEQS, SEQS)].rearrange("b t c -> t b c"), y).then_inc(s.x_stored, 16)

            load(p, d["x"], 0)
            for dst, src in LOADS[:LOADS_P]:
                sp.dma_start(dst, src).then_inc(loaded_p, 16)
            for dst, src in LOADS[LOADS_P:]:
                sp.dma_start(dst, src).then_inc(loaded_q, 16)
            C.section = "A"
            with sp.Fori(1, NGROUPS) as it:
                sp.wait_ge(p_free, C.next(p_free))
                load(p, d["x"], it)
                sp.wait_ge(x_ready, C.next(x_ready))
                store(q, q.hres[:], it - 1)
                C.settle(sp, p_free)
                C.settle(sp, x_ready)
            C.section = "A, last"
            sp.wait_ge(x_ready, C.next(x_ready))
            store(q, q.hres[:], NGROUPS - 1)
            C.settle(sp, x_ready)
            sp.wait_ge(x_safe, 1)
            for s in streams:
                load(s, out, s.index)
            C.section = "C"
            with sp.Fori(1, NGROUPS // 2) as it:
                for s in streams:
                    sp.wait_ge(s.x_done, C.next(s.x_done))
                    store(s, s.n[:], it * 2 + (s.index - 2))
                    C.settle(sp, s.x_done)
                    load(s, out, it * 2 + s.index)
            for s in streams:
                sp.wait_ge(s.x_done, 1)
                store(s, s.n[:], NGROUPS - 2 + s.index)

        @block.gpsimd
        def _(pool):
            k = [0]

            def done(ins):
                k[0] += 1
                ins.then_inc(consts, 1)
                pool.wait_ge(consts, k[0])
            done(pool.memset(ident[:], 0.0))
            done(pool.affine_select(out=ident[:], in_=ident[:], compare_op=ALU.not_equal, fill=1.0, base=0,
                                    pattern=[[-1, 128]], channel_multiplier=1))
            done(pool.tensor_copy(identb[:], ident[:]))
            done(pool.memset(causal[:], 0.0))
            done(pool.affine_select(out=causal[:], in_=causal[:], compare_op=ALU.is_ge, fill=-BIG, base=0,
                                    pattern=[[0, 4], [-1, 128]], channel_multiplier=1))
            done(pool.memset(diag[:], 1.0))
            done(pool.affine_select(out=diag[:], in_=diag[:], compare_op=ALU.is_ge, fill=0.0, base=0,
                                    pattern=[[-8, 4], [-32, 4]], channel_multiplier=1))
            done(pool.affine_select(out=diag[:], in_=diag[:], compare_op=ALU.is_ge, fill=0.0, base=7,
                                    pattern=[[8, 4], [32, 4]], channel_multiplier=-1))
            done(pool.tensor_tensor(subscale[:], diag[:, :, 0], diag[:, :, 1], ALU.add))
            done(pool.tensor_tensor(subone[:], diag[:, :, 2], diag[:, :, 3], ALU.add))
            done(pool.tensor_tensor(subone[:], subone[:], subscale[:], ALU.add))
            done(pool.tensor_scalar(subscale[:], subone[:], float(HDIM) ** -0.5, None, ALU.mult))
            done(pool.iota(rank5[:], pattern=[[0, 2 * SH * SEQS], [-1, SE]], base=SE, channel_multiplier=0,
                           allow_small_or_imprecise_dtypes=True))
            done(pool.iota(rank8[:], pattern=[[0, SEQS], [-1, ME]], base=ME, channel_multiplier=0,
                           allow_small_or_imprecise_dtypes=True))
            done(pool.memset(minushalf[:], -0.5))
            assert k[0] == NCONST

            def rsqrt(s, eps):
                pool.wait_ge(s.var_ready, C.next(s.var_ready))
                pool.tensor_scalar(s.rstd[:], s.mv[:, :, 1], eps, None, ALU.add).then_inc(C.give(pool_step), 1)
                pool.wait_ge(pool_step, C.next(pool_step))
                pool.tensor_tensor(s.rstd[:], s.rstd[:], minushalf[:], ALU.pow).then_inc(C.give(s.rstd_ready), 1)

            def gated_values(s, b):
                for ex in range(SE):
                    yield
                    dst = s.prod if ex else s.vs[:, b, :]
                    pool.tensor_tensor(
                        dst.rearrange("p (h k) -> p h k", h=SH),
                        s.xvs[:, b, ex * SHD:(ex + 1) * SHD].unsqueeze(1).broadcast_to([128, SH, SHD]),
                        s.gates[:, b, 0:SH, ex].unsqueeze(2).broadcast_to([128, SH, SHD]),
                        ALU.mult).then_inc(C.give(pool_step), 1)
                    pool.wait_ge(pool_step, C.next(pool_step))
                    if ex:
                        ins = pool.tensor_tensor(s.vs[:, b, :], s.vs[:, b, :], s.prod, ALU.add)
                        if ex < SE - 1:
                            ins.then_inc(C.give(pool_step), 1)
                            pool.wait_ge(pool_step, C.next(pool_step))
                        else:
                            ins.then_inc(C.give(s.v_gated), 1)

            def gated_outputs(s, b):
                pool.wait_ge(s.ogate_ready, C.next(s.ogate_ready))
                pool.wait_ge(s.av_pool, C.next(s.av_pool))
                pool.wait_ge(oprod_free, C.next(oprod_free))
                for ex in range(POOL_OUT):
                    ins = pool.tensor_tensor(
                        oprod[:, ex, :].rearrange("p (h k) -> p h k", h=SH),
                        s.av[:, b % 2, :].rearrange("p (h k) -> p h k", h=SH),
                        s.gates[:, b, SH:, ex].unsqueeze(2).broadcast_to([128, SH, SHD]), ALU.mult)
                ins.then_inc(C.give(oprod_ready), 1)

            def layers_p(s):
                yield
                rsqrt(s, LN_EPS)
                yield
                rsqrt(s, LN_EPS)
                yield
                pool.wait_ge(s.gate_ready, C.next(s.gate_ready))
                pool.drain()
                yield from gated_values(s, 0)
                yield from gated_values(s, 1)
                for b in range(SEQS):
                    yield
                    gated_outputs(s, b)
                    if b + 2 < SEQS:
                        yield from gated_values(s, b + 2)

            def layers_q(s):
                yield
                rsqrt(s, LN_EPS)
                yield
                rsqrt(s, LN_EPS)
                yield
                rsqrt(s, RMS_EPS)
                yield
                rsqrt(s, RMS_EPS)
                yield
                rsqrt(s, LN_EPS)
                yield
                rsqrt(s, LN_EPS)

            def layers_c(s):
                yield
                rsqrt(s, LN_EPS)
                yield
                rsqrt(s, LN_EPS)

            def settle(*sems):
                for each in (*sems, pool_step):
                    C.settle(pool, each)

            C.section = "A, first"
            alone(layers_p(p))
            settle(p.var_ready, p.gate_ready, p.ogate_ready, p.av_pool, oprod_free)
            C.section = "A"
            with pool.Fori(1, NGROUPS) as it:
                in_order(ORDER["A", "gpsimd"], layers_p(p), layers_q(q))
                settle(p.var_ready, p.gate_ready, p.ogate_ready, p.av_pool, oprod_free, q.var_ready)
            C.section = "A, last"
            alone(layers_q(q))
            settle(q.var_ready)
            for i in range(2):
                pool.wait_ge(amax_ready, i + 1)
                pool.partition_all_reduce(gmax[:, 2 * i + 1:2 * i + 2], gmax[:, 2 * i:2 * i + 1], 128,
                                          bass.bass_isa.ReduceOp.max).then_inc(gmax_ready, 1)
            C.section = "C"
            with pool.Fori(0, NGROUPS // 2) as it:
                in_order(ORDER["C", "gpsimd"], layers_c(p), layers_c(q))
                settle(p.var_ready, q.var_ready)

        @block.tensor
        def _(pe):
            pe.wait_ge(loaded_p, NLOAD_P)
            pe.wait_ge(consts, NCONST)

            def settle(s, *sems):
                for ring in (s.pe_a, s.pe_d, s.pe_s):
                    if ring.taken:
                        assert ring.taken % len(ring.banks) == 0
                        C.settle(pe, ring.drained, ring.taken)
                        ring.taken = 0
                for each in sems:
                    C.settle(pe, each)

            mm = pe.matmul

            def tokens(b):
                return slice(b * TOK, (b + 1) * TOK)

            def transpose_n(s):
                pe.wait_ge(s.n_ready, C.next(s.n_ready))
                pe.wait_ge(s.a_drained, s.pe_a.take())
                o = s.pe_a.bank
                for b in range(SEQS):
                    ins = pe.transpose(o[:, tokens(b)], s.n[:, b, :], ident[:])
                ins.then_inc(C.give(s.a_full), 1)
                return s.pe_a.item()

            def transpose_ctx(s):
                pe.wait_ge(s.ctx_in, 16)
                pe.sem_inc(s.ctx_in, -16)
                pe.wait_ge(s.a_drained, s.pe_a.take())
                o = s.pe_a.bank
                for b in range(SEQS):
                    ins = pe.transpose(o[:, b * CTX:(b + 1) * CTX], s.ctxg[:, b, :], ident[0:CTX, 0:CTX])
                ins.then_inc(C.give(s.a_full), 1)
                return s.pe_a.item()

            def project(ring, w, src):
                pe.wait_ge(ring.drained, ring.take())
                o = ring.bank
                mm(o[0:w.shape[1], 0:src.shape[1]], w, src, start=True, stop=True).then_inc(C.give(ring.full), 1)
                return ring.item()

            def values(ring, w, src, rows=TOK):
                pe.wait_ge(ring.drained, ring.take())
                o = ring.bank
                cols = w.shape[1]
                for b in range(SEQS):
                    ins = mm(o[0:rows, b * cols:(b + 1) * cols], src(b), w, start=True, stop=True)
                ins.then_inc(C.give(ring.full), 1)
                return ring.item()

            def heads_out(s, w):
                return values(s.pe_d, w, lambda b: s.aT[:, tokens(b)])

            def add_heads(s, o, b, j, rows, rhs):
                for g in range(QUADS):
                    ins = mm(o[32 * g:32 * g + 32, tokens(b)], s.vdiag[0:rows, b, g, 32 * j:32 * j + 32],
                             rhs(g), start=(j == 0), stop=(j == SUBS - 1))
                return ins

            def causal_heads(s, keys, w_out, q_item, k_item, v_item):
                units = [(b, j) for b in range(SEQS) for j in range(SUBS)]
                s_items, t_items = {}, {}
                o = None
                for u in range(len(units) + LAG_V):
                    yield
                    if u == 0:
                        pe.wait_ge(s.d_drained, q_item)
                        pe.wait_ge(s.a_drained, k_item)
                    if u < len(units):
                        b, j = units[u]
                        pe.wait_ge(s.s_drained, s.pe_s.take())
                        o_s = s.pe_s.bank[:, 0:4 * keys].rearrange("p (g k) -> p g k", g=QUADS)
                        mm(o_s, s.sub_rows[:, b, j, :], s.quad_rows[:, b, :, 0:keys], start=True, stop=False)
                        mm(o_s, identb[:], causal[:, :, 0:keys], start=False, stop=True).then_inc(C.give(s.s_full), 1)
                        s_items[u] = s.pe_s.item()
                    v = u - LAG_T
                    if 0 <= v < len(units):
                        yield
                        pe.wait_ge(s.a_drained, s.pe_a.take())
                        t = s.pe_a.bank
                        pe.wait_ge(s.s_drained, s_items[v])
                        for g in range(QUADS):
                            ins = pe.transpose(t[0:keys, tokens(g)], s.e[:, v % 4, g * keys:(g + 1) * keys], ident[:])
                        ins.then_inc(C.give(s.a_full), 1)
                        t_items[v] = s.pe_a.item()
                    v = u - LAG_V
                    if 0 <= v < len(units):
                        yield
                        b, j = units[v]
                        if v == 0:
                            pe.wait_ge(s.d_drained, s.pe_d.take())
                            o = s.pe_d.bank
                            pe.wait_ge(s.d_drained, v_item)
                        pe.wait_ge(s.a_drained, t_items[v])
                        ins = add_heads(s, o, b, j, keys, lambda g: s.eT[0:keys, v % 2, tokens(g)])
                ins.then_inc(C.give(s.d_full), 1)
                heads_item = s.pe_d.item()
                yield
                pe.wait_ge(s.rz_ready, C.next(s.rz_ready))
                pe.wait_ge(s.a_drained, s.pe_a.take())
                t = s.pe_a.bank
                for b in range(SEQS):
                    ins = pe.transpose(t[0:16, tokens(b)], s.rz[:, b, :], ident[:])
                ins.then_inc(C.give(s.a_full), 1)
                yield
                pe.wait_ge(s.a_drained, s.pe_a.item())
                project(s.pe_a, headsel[:], s.rzT[:])
                yield
                pe.wait_ge(s.d_drained, heads_item)
                heads_out(s, w_out)

            def transpose_p(s):
                pe.wait_ge(s.p_ready, C.next(s.p_ready))
                pe.wait_ge(s.a_drained, s.pe_a.take())
                t = s.pe_a.bank
                for b in range(SEQS):
                    ins = pe.transpose(t[0:CTX, tokens(b)], s.work[:, b, :], ident[:])
                ins.then_inc(C.give(s.a_full), 1)
                return s.pe_a.item()

            def weights():
                for w in range(2):
                    yield
                    pe.wait_ge(w_ready, C.next(w_ready))
                    pe.wait_ge(q.a_drained, q.pe_a.take())
                    o = q.pe_a.bank
                    for t, (r0, m) in enumerate(ITILES):
                        ins = pe.transpose(o[:, r0:r0 + m], wraw[0:m, w, t, :], ident[0:m, 0:m])
                    ins.then_inc(C.give(q.a_full), 1)
                yield
                pe.wait_ge(w_ready, C.next(w_ready))
                pe.wait_ge(q.a_drained, q.pe_a.take())
                o = q.pe_a.bank
                for t, (r0, m) in enumerate(ITILES):
                    pe.transpose(o[0:m, t * 128:(t + 1) * 128], wdraw[:, r0:r0 + m], ident[:])
                pe.transpose(o[0:16, 384:512], diag[:, :, :].rearrange("p j g -> p (j g)"), ident[:])\
                    .then_inc(C.give(q.a_full), 1)
                yield
                pe.wait_ge(w_ready, C.next(w_ready))
                project(q.pe_a, dscaleB[:], ident[:])
            def layers_p(s):
                yield
                ctx_item = transpose_ctx(s)
                yield
                pe.wait_ge(s.a_drained, ctx_item)
                k_item = project(s.pe_d, w0k[:], s.ctxT2)
                yield
                n_item = transpose_n(s)
                yield
                v_item = values(s.pe_d, w0v[:], lambda b: s.ctxT[:, b, :], CTX)
                yield
                pe.wait_ge(s.a_drained, n_item)
                q_item = project(s.pe_a, w0q[:], s.nT[:])
                s_items = {}
                for place, kind, u in L0X_STEPS:
                    yield
                    b, j = divmod(u, SUBS)
                    if kind == "scores":
                        if u == 0:
                            pe.wait_ge(s.d_drained, v_item)
                            pe.wait_ge(s.a_drained, q_item)
                        pe.wait_ge(s.s_drained, s.pe_s.take())
                        o_s = s.pe_s.bank[0:CTX, :].rearrange("p (g t) -> p g t", g=QUADS)
                        mm(o_s, s.sub_rows[:, b, j, 0:CTX], s.quad_rows[:, b, :, :],
                           start=True, stop=True).then_inc(C.give(s.s_full), 1)
                        s_items[u] = s.pe_s.item()
                    else:
                        if u == 0:
                            pe.wait_ge(s.a_drained, s.pe_a.take())
                            o = s.pe_a.bank
                        if j == 0:
                            pe.wait_ge(s.v_ready, C.next(s.v_ready))
                            pe.wait_ge(s.s_drained, s_items[u + SUBS - 1])
                        ins = add_heads(s, o, b, j, CTX, lambda g: s.e[0:CTX, j, tokens(g)])
                        if b < SEQS - 1:
                            ins.then_inc(C.give(s.e_used), 1)
                ins.then_inc(C.give(s.a_full), 1)
                yield
                pe.wait_ge(s.a_drained, s.pe_a.item())
                heads_out(s, w0o[:])

                yield
                n_item = transpose_n(s)
                yield
                for b in range(SEQS):
                    yield
                    if b == 0:
                        pe.wait_ge(s.a_drained, n_item)
                    pe.wait_ge(s.a_drained, s.pe_a.take())
                    o = s.pe_a.bank
                    mm(o[:, 0:NV + 2 * NGATE], s.nT[:, tokens(b)], wsv[:], start=True, stop=True).then_inc(C.give(s.a_full), 1)
                for t in range(4):
                    yield
                    q_item = project(s.pe_a, wsq[:, t * 128:(t + 1) * 128], s.nT[:])
                    k_item = project(s.pe_s, wsk[:, t * 128:(t + 1) * 128], s.nT[:])
                units = [(b, p) for b in range(SEQS) for p in range(2)]
                s_items, t_items = {}, {}
                for u in range(len(units) + LAG_V):
                    yield
                    if u == 0:
                        pe.wait_ge(s.a_drained, q_item)
                        pe.wait_ge(s.s_drained, k_item)
                    if u < len(units):
                        b, p = units[u]
                        pe.wait_ge(s.s_drained, s.pe_s.take())
                        o_s = s.pe_s.bank
                        for t in range(4):
                            ins = mm(o_s[:, tokens(t)], s.qf[64 * p:64 * p + 64, t, tokens(b)],
                                     s.kf[64 * p:64 * p + 64, t, tokens(b)], start=True, stop=True)
                        ins.then_inc(C.give(s.s_full), 1)
                        s_items[u] = s.pe_s.item()
                    v = u - LAG_V
                    if v >= 0 and v % 2 == 1 and v < len(units):
                        yield
                        b = v // 2
                        pe.wait_ge(s.a_drained, s.pe_a.take())
                        o = s.pe_a.bank
                        pe.wait_ge(s.v_gated, C.next(s.v_gated))
                        pe.wait_ge(s.a_drained, t_items[v])
                        for p in range(2):
                            for t in range(4):
                                h = 2 * t + p
                                ins = mm(o[:, h * SHD:(h + 1) * SHD], s.eT[:, p, tokens(t)],
                                         s.vs[:, b, h * SHD:(h + 1) * SHD], start=True, stop=True)
                        ins.then_inc(C.give(s.a_full), 1)
                    v = u - LAG_T
                    if 0 <= v < len(units):
                        yield
                        pe.wait_ge(s.a_drained, s.pe_a.take())
                        tb = s.pe_a.bank
                        pe.wait_ge(s.s_drained, s_items[v])
                        for t in range(4):
                            ins = pe.transpose(tb[:, tokens(t)], s.e[:, v % 4, tokens(t)], ident[:])
                        ins.then_inc(C.give(s.a_full), 1)
                        t_items[v] = s.pe_a.item()
                for t in range(3):
                    yield
                    if t == 0:
                        pe.wait_ge(s.y_ready, C.next(s.y_ready))
                    rows = min(128, NV - 128 * t)
                    pe.wait_ge(s.a_drained, s.pe_a.take())
                    tb = s.pe_a.bank
                    for b in range(SEQS):
                        ins = pe.transpose(tb[0:rows, tokens(b)], s.ys[:, b, 128 * t:128 * t + rows], ident[:])
                    ins.then_inc(C.give(s.a_full), 1)
                yield
                pe.wait_ge(s.d_drained, s.pe_d.take())
                o = s.pe_d.bank
                pe.wait_ge(s.a_drained, s.pe_a.item())
                for b in range(SEQS):
                    for t in range(3):
                        rows = min(128, NV - 128 * t)
                        ins = mm(o[:, tokens(b)], s.ysT[0:rows, t, tokens(b)], wso[0:rows, t, :],
                                 start=(t == 0), stop=(t == 2))
                ins.then_inc(C.give(s.d_full), 1)

            def layers_q(s):
                def nTb(b):
                    return s.nT[:, tokens(b)]

                yield
                pe.wait_ge(handed, C.next(handed))
                project(s.pe_a, w1k[:], s.ctxT2)
                v_item = values(s.pe_d, w1v[:], lambda b: s.ctxT[:, b, :], CTX)
                yield
                n_item = transpose_n(s)
                yield
                pe.wait_ge(s.a_drained, n_item)
                q_item = project(s.pe_a, w1q[:], s.nT[:])
                yield
                pe.wait_ge(s.d_drained, v_item)
                pe.wait_ge(s.a_drained, q_item)
                pe.wait_ge(s.d_drained, s.pe_d.take())
                o = s.pe_d.bank
                for b in range(SEQS):
                    ins = mm(o[:, b * CTX:(b + 1) * CTX], s.q1[:, tokens(b)], s.kf[:, 0, b * CTX:(b + 1) * CTX],
                             start=True, stop=True)
                ins.then_inc(C.give(s.d_full), 1)
                yield
                p_item = transpose_p(s)
                yield
                pe.wait_ge(s.a_drained, p_item)
                pe.wait_ge(s.a_drained, s.pe_a.take())
                o = s.pe_a.bank
                for b in range(SEQS):
                    ins = mm(o[:, tokens(b)], s.vg[0:CTX, b, :], s.eT[0:CTX, 0, tokens(b)], start=True, stop=True)
                ins.then_inc(C.give(s.a_full), 1)
                yield
                pe.wait_ge(s.a_drained, s.pe_a.item())
                heads_out(s, w1o[:])

                yield
                n_item = transpose_n(s)
                yield
                pe.wait_ge(s.a_drained, n_item)
                k_item = project(s.pe_a, wgk[:], s.nT[:])
                q_item = project(s.pe_d, wgq[:], s.nT[:])
                yield
                v_item = values(s.pe_d, wgv[:], nTb)
                yield from causal_heads(s, TOK, wgo[:], q_item, k_item, v_item)
                yield
                n_item = transpose_n(s)
                yield
                pe.wait_ge(s.a_drained, n_item)
                values(s.pe_d, wgate[:], nTb)
                for i in range(2 * SEQS):
                    b, half = divmod(i, 2)
                    yield
                    pe.wait_ge(s.s_drained, s.pe_s.take())
                    o = s.pe_s.bank
                    mm(o[:], nTb(b), wexp[:, half * 512:(half + 1) * 512], start=True, stop=True)\
                        .then_inc(C.give(s.s_full), 1)

                yield
                n_item = transpose_n(s)
                yield
                pe.wait_ge(s.a_drained, n_item)
                pe.wait_ge(s.d_drained, s.pe_d.take())
                o = s.pe_d.bank
                for b in range(SEQS):
                    ins = mm(o[:, b * CTX:(b + 1) * CTX], nTb(b), s.ctxT[:, b, :], start=True, stop=True)
                ins.then_inc(C.give(s.d_full), 1)
                yield
                p_item = transpose_p(s)
                yield
                pe.wait_ge(s.a_drained, p_item)
                pe.wait_ge(s.d_drained, s.pe_d.take())
                o = s.pe_d.bank
                for b in range(SEQS):
                    ins = mm(o[:, tokens(b)], s.eT[0:CTX, 0, tokens(b)], s.ctxg[:, b, :], start=True, stop=True)
                ins.then_inc(C.give(s.d_full), 1)
                yield
                transpose_n(s)
                pe.drain().then_inc(C.give(s.n_read), 1)

            C.section = "A, first"
            in_order(ORDER["first", "tensor"], layers_p(p), weights())
            settle(p, p.n_ready, p.v_ready, p.v_gated, p.y_ready)
            settle(q, w_ready)
            C.section = "A"
            with pe.Fori(1, NGROUPS) as it:
                in_order(ORDER["A", "tensor"], layers_p(p), layers_q(q))
                settle(p, p.n_ready, p.v_ready, p.v_gated, p.y_ready)
                settle(q, q.n_ready, q.rz_ready, q.p_ready, handed)
            C.section = "A, last"
            alone(layers_q(q))
            settle(q, q.n_ready, q.rz_ready, q.p_ready, handed)

            def layers_b(s):
                for t, (r0, m) in enumerate(ITILES):
                    yield
                    if t == 0:
                        pe.wait_ge(s.q_ready, C.next(s.q_ready))
                    project(s.pe_a, wgu[:, 0, r0:r0 + m], s.xq[:])
                    project(s.pe_d, wgu[:, 1, r0:r0 + m], s.xq[:])

            C.section = "B"
            with pe.Fori(0, NGROUPS // 2) as it:
                in_order(ORDER["B", "tensor"], layers_b(p), layers_b(q))
                for s in streams:
                    settle(s, s.q_ready)

            def layers_c(s):
                yield
                ctx_item = transpose_ctx(s)
                yield
                pe.wait_ge(s.a_drained, ctx_item)
                k_item = project(s.pe_a, w3k[:], s.ctxT2)
                pe.wait_ge(s.q_ready, C.next(s.q_ready))
                pe.wait_ge(s.d_drained, s.pe_d.take())
                o = s.pe_d.bank
                for b in range(SEQS):
                    for t, (r0, m) in enumerate(ITILES):
                        ins = mm(o[:, tokens(b)], s.hq[0:m, t, tokens(b)], wdq[0:m, t, :],
                                 start=(t == 0), stop=(t == 2))
                ins.then_inc(C.give(s.d_full), 1)
                yield
                v_item = values(s.pe_d, w3v[:], lambda b: s.ctxT[:, b, :], CTX)
                yield
                n_item = transpose_n(s)
                yield
                pe.wait_ge(s.a_drained, n_item)
                q_item = project(s.pe_d, w3q[:], s.nT[:])
                yield from causal_heads(s, CTX, w3o[:], q_item, k_item, v_item)
                yield
                n_item = transpose_n(s)
                yield
                for t in range(4):
                    yield
                    if t == 0:
                        pe.wait_ge(s.a_drained, n_item)
                    ring = s.pe_d if t % 2 else s.pe_a
                    project(ring, w31[:, t * 128:(t + 1) * 128], s.nT[:])
                yield
                pe.wait_ge(s.a_drained, s.pe_a.item())
                pe.wait_ge(s.d_drained, s.pe_d.take())
                o = s.pe_d.bank
                for b in range(SEQS):
                    for t in range(4):
                        ins = mm(o[:, tokens(b)], s.hid[:, t, tokens(b)], w32[:, t, :], start=(t == 0), stop=(t == 3))
                ins.then_inc(C.give(s.d_full), 1)

            C.section = "C"
            with pe.Fori(0, NGROUPS // 2) as it:
                in_order(ORDER["C", "tensor"], layers_c(p), layers_c(q))
                for s in streams:
                    settle(s, s.n_ready, s.q_ready, s.rz_ready)

        @block.scalar
        def _(act):
            act.wait_ge(loaded_p, NLOAD_P)
            act.wait_ge(consts, NCONST)
            act.wait_ge(zeroed, 1)

            def copy(dst, src, bias=0.0, scale=1.0, func=ACT.Identity):
                return act.activation(dst, src, func, bias=bias, scale=scale)

            def settle(s, *sems):
                if s.act_a.taken:
                    C.settle(act, s.a_full, s.act_a.taken)
                s.act_a.taken = s.act_s.taken = 0
                for each in sems:
                    C.settle(act, each)

            def take_n(s, scale=1.0):
                act.wait_ge(s.a_full, s.act_a.take())
                copy(s.nT[:], s.act_a.bank[:, 0:SEQS * TOK], scale=scale).then_inc(C.give(s.a_drained), 1)

            def take_ctx(s):
                act.wait_ge(s.a_full, s.act_a.take())
                copy(s.ctxT2, s.act_a.bank[:, 0:SEQS * CTX]).then_inc(C.give(s.a_drained), 1)

            def take_quads(s, cols, bias=None):
                act.wait_ge(s.a_full, s.act_a.take())
                o = s.act_a.bank
                for g in range(QUADS):
                    p = slice(32 * g, 32 * g + 32)
                    ins = copy(s.quad_rows[p, :, g, 0:cols], o[p, 0:SEQS * cols].rearrange("p (b t) -> p b t", b=SEQS),
                               bias=bias[p, :] if bias is not None else 0.0)
                ins.then_inc(C.give(s.a_drained), 1)

            def exps(s, rows, width, b, j, u, sums=True):
                act.wait_ge(s.max_ready, C.next(s.max_ready))
                s.act_s.take()
                o = s.act_s.bank
                for g in range(4):
                    head = 4 * j + g
                    ins = act.activation(s.e[0:rows, u % 4, g * width:(g + 1) * width], o[0:rows, g * width:(g + 1) * width],
                                         ACT.Exp, bias=s.negmax[0:rows, b, head:head + 1],
                                         accum_out=s.zsum[0:rows, b, head:head + 1] if sums else None)
                ins.then_inc(C.give(s.s_drained), 1)

            def sums_done(s):
                act.drain().then_inc(C.give(s.sums_ready), 1)

            def causal_heads(s, keys, act_sums):
                n_units = SEQS * SUBS
                for u in range(n_units + LAG_T):
                    yield
                    if u < n_units:
                        exps(s, TOK, keys, u // SUBS, u % SUBS, u, sums=act_sums)
                        if not act_sums:
                            act.drain().then_inc(C.give(s.e_ready), 1)
                        elif u == n_units - 1:
                            sums_done(s)
                    v = u - LAG_T
                    if 0 <= v:
                        yield
                        act.wait_ge(s.a_full, s.act_a.take())
                        copy(s.eT[0:keys, v % 2, :], s.act_a.bank[0:keys, :]).then_inc(C.give(s.a_drained), 1)
                yield
                act.wait_ge(s.a_full, s.act_a.take())
                copy(s.rzT[:], s.act_a.bank[0:16, 0:SEQS * TOK]).then_inc(C.give(s.a_drained), 1)
                yield
                act.wait_ge(s.a_full, s.act_a.take())
                copy(s.rzB[:], s.act_a.bank[:, 0:SEQS * TOK]).then_inc(C.give(s.a_drained), 1)
                act.drain().then_inc(C.give(s.rzB_ready), 1)

            def exp_p(s):
                yield
                act.wait_ge(s.pmax_ready, C.next(s.pmax_ready))
                for b in range(SEQS):
                    ins = act.activation(s.e[:, 0, b * CTX:(b + 1) * CTX], s.sc[:, b, :], ACT.Exp, bias=s.negmax[:, b, 0:1])
                ins.then_inc(C.give(s.pexp_ready), 1)
                yield
                act.wait_ge(s.a_full, s.act_a.take())
                copy(s.eT[0:CTX, 0, 0:SEQS * TOK], s.act_a.bank[0:CTX, 0:SEQS * TOK]).then_inc(C.give(s.a_drained), 1)

            def weights():
                yield
                act.wait_ge(q.a_full, q.act_a.take())
                copy(wgu[:, 0, 0:INNER], q.act_a.bank[:, 0:INNER]).then_inc(C.give(q.a_drained), 1)
                yield
                act.wait_ge(q.a_full, q.act_a.take())
                copy(wgu[:, 1, 0:INNER], q.act_a.bank[:, 0:INNER]).then_inc(C.give(q.a_drained), 1)
                yield
                act.wait_ge(q.a_full, q.act_a.take())
                o = q.act_a.bank
                copy(wdq[:, 0:2, :], o[:, 0:256].rearrange("p (t c) -> p t c", t=2))
                copy(wdq[0:96, 2, :], o[0:96, 256:384])
                copy(headsel[:], o[0:16, 384:512]).then_inc(C.give(q.a_drained), 1)
                yield
                act.wait_ge(q.a_full, q.act_a.take())
                copy(dscaleB[:], q.act_a.bank[:, 0:128]).then_inc(C.give(q.a_drained), 1)
                act.activation(clipe[:], clips[:], ACT.Exp, scale=-1.0).then_inc(clip_exp, 1)
            def layers_p(s):
                yield
                take_ctx(s)
                yield
                take_n(s)
                yield
                take_quads(s, TOK, b0q)
                for place, kind, u in L0X_STEPS:
                    if kind == "scores":
                        yield
                        if u >= SUBS:
                            act.wait_ge(s.e_used, C.next(s.e_used))
                        exps(s, CTX, TOK, u // SUBS, u % SUBS, u)
                        if u % SUBS == SUBS - 1:
                            sums_done(s)
                yield
                act.wait_ge(s.a_full, s.act_a.take())
                copy(s.aT[:], s.act_a.bank[:, 0:SEQS * TOK]).then_inc(C.give(s.a_drained), 1)
                yield
                take_n(s)
                for b in range(SEQS):
                    yield
                    act.wait_ge(s.a_full, s.act_a.take())
                    copy(s.xvs[:, b, :], s.act_a.bank[:, 0:NV + 2 * NGATE]).then_inc(C.give(s.a_drained), 1)
                act.drain().then_inc(C.give(s.xv_ready), 1)
                act.activation(s.gexp[:, :, :, :].rearrange("p b h e -> p b (h e)"), s.xvs[:, :, NV:NV + NGATE], ACT.Exp,
                               scale=-1.0).then_inc(C.give(s.sig_ready), 1)
                for t in range(4):
                    yield
                    act.wait_ge(s.a_full, s.act_a.take())
                    copy(s.qf[:, t, :], s.act_a.bank[:, 0:SEQS * TOK], scale=float(SHD) ** -0.5)\
                        .then_inc(C.give(s.a_drained), 1)
                n_units = 2 * SEQS
                for u in range(n_units + LAG_V):
                    yield
                    if u < n_units:
                        exps(s, TOK, TOK, u // 2, u % 2, u)
                        if u % 2 == 1:
                            sums_done(s)
                    v = u - LAG_V
                    if v >= 0 and v % 2 == 1 and v < n_units:
                        yield
                        act.wait_ge(s.a_full, s.act_a.take())
                        copy(s.av[:, v // 2 % 2, :], s.act_a.bank[:]).then_inc(C.give(s.a_drained), 1)
                        act.drain().then_inc(C.give(s.av_dve), 1)
                        act.drain().then_inc(C.give(s.av_pool), 1)
                    v = u - LAG_T
                    if 0 <= v < n_units:
                        yield
                        act.wait_ge(s.a_full, s.act_a.take())
                        copy(s.eT[:, v % 2, :], s.act_a.bank[:]).then_inc(C.give(s.a_drained), 1)
                for t in range(3):
                    yield
                    rows = min(128, NV - 128 * t)
                    act.wait_ge(s.a_full, s.act_a.take())
                    copy(s.ysT[0:rows, t, :], s.act_a.bank[0:rows, 0:SEQS * TOK]).then_inc(C.give(s.a_drained), 1)
            def layers_q(s, it):
                yield
                act.wait_ge(s.a_full, s.act_a.take())
                copy(s.kf[:, 0, 0:SEQS * CTX], s.act_a.bank[:, 0:SEQS * CTX], bias=b1k[:]).then_inc(C.give(s.a_drained), 1)
                yield
                take_n(s)
                yield
                act.wait_ge(s.a_full, s.act_a.take())
                copy(s.q1[:], s.act_a.bank[:, 0:SEQS * TOK], bias=b1q[:]).then_inc(C.give(s.a_drained), 1)
                yield from exp_p(s)
                yield
                act.wait_ge(s.a_full, s.act_a.take())
                copy(s.aT[:], s.act_a.bank[:, 0:SEQS * TOK], bias=b1v[:]).then_inc(C.give(s.a_drained), 1)
                yield
                take_n(s, scale=attn_w[:])
                yield
                take_quads(s, TOK)
                yield from causal_heads(s, TOK, act_sums=True)
                yield
                take_n(s, scale=ffn_w[:])
                yield
                act.wait_ge(s.c_ready, C.next(s.c_ready))
                act.activation(s.clog[:], s.clog[:], ACT.Exp).then_inc(C.give(s.cexp_ready), 1)
                yield
                take_n(s)
                yield from exp_p(s)
                yield
                act.wait_ge(s.a_full, s.act_a.take())
                copy(nT_all[:, bass.ds(it * SEQS * TOK, SEQS * TOK)], s.act_a.bank[:, 0:SEQS * TOK]).then_inc(C.give(s.a_drained), 1)

            C.section = "A, first"
            in_order(ORDER["first", "scalar"], layers_p(p), weights())
            settle(p, p.max_ready, p.e_used)
            settle(q)
            C.section = "A"
            with act.Fori(1, NGROUPS) as it:
                in_order(ORDER["A", "scalar"], layers_p(p), layers_q(q, it - 1))
                settle(p, p.max_ready, p.e_used)
                settle(q, q.max_ready, q.pmax_ready, q.c_ready)
            C.section = "A, last"
            alone(layers_q(q, NGROUPS - 1))
            settle(q, q.max_ready, q.pmax_ready, q.c_ready)

            def layers_b(s):
                for t, (r0, m) in enumerate(ITILES):
                    yield
                    act.wait_ge(s.a_full, s.act_a.take())
                    act.activation(s.eT[0:m, t % 2, :], s.act_a.bank[0:m, :], ACT.Silu, scale=actscale[0:m, t:t + 1])\
                        .then_inc(C.give(s.a_drained), 1)
                    act.drain().then_inc(C.give(s.sil_ready), 1)

            C.section = "B"
            act.wait_ge(sx_ready, 1)
            with act.Fori(0, NGROUPS // 2) as it:
                in_order(ORDER["B", "scalar"], layers_b(p), layers_b(q))
                for s in streams:
                    settle(s)

            def layers_c(s):
                yield
                take_ctx(s)
                yield
                take_quads(s, CTX)
                yield
                take_n(s)
                yield from causal_heads(s, CTX, act_sums=False)
                yield
                take_n(s)
                for t in (0, 2):
                    yield
                    act.wait_ge(s.a_full, s.act_a.take())
                    act.activation(s.hid[:, t, :], s.act_a.bank[:, 0:SEQS * TOK], ACT.Relu, bias=b31[:, t:t + 1])\
                        .then_inc(C.give(s.a_drained), 1)

            C.section = "C"
            with act.Fori(0, NGROUPS // 2) as it:
                in_order(ORDER["C", "scalar"], layers_c(p), layers_c(q))
                for s in streams:
                    settle(s, s.max_ready)

        @block.vector
        def _(dve):
            dve.sem_inc(oprod_free, 1)
            for s in streams:
                dve.sem_inc(s.a_drained, 1)
                dve.sem_inc(s.d_drained, 1)
                dve.sem_inc(s.s_drained, 2)
            dve.sem_inc(q.n_read, 1)
            dve.sem_inc(q.x_stored, 16)
            for s in streams:
                dve.memset(s.quad_rows[:], 0.0)
                dve.memset(s.vdiag[:], 0.0)
            dve.memset(hmax[:], 0.0)
            dve.drain().then_inc(zeroed, 1)
            dve.wait_ge(loaded_p, NLOAD_P)
            dve.wait_ge(consts, NCONST)

            def settle(s, *sems):
                for each in sems:
                    C.settle(dve, each)
                for ring in (s.dve_d, s.dve_s):
                    if ring.taken:
                        C.settle(dve, ring.full, ring.taken)
                s.dve_d.taken = s.dve_s.taken = 0

            def settle_steps():
                dve.wait_ge(dve_step, C.last(dve_step))
                C.settle(dve, dve_step)

            tt, ts, stt = dve.tensor_tensor, dve.tensor_scalar, dve.scalar_tensor_tensor

            def reduce(dst, src, op, **kw):
                return dve.tensor_reduce(dst, src, X, op, **kw)

            def by_seq(bank):
                return bank[:, 0:SEQS * CH].rearrange("p (b c) -> p b c", b=SEQS)

            def softmax_scale(s, probs):
                reduce(s.z1[:], probs, ALU.add).then_inc(C.give(dve_step), 1)
                dve.wait_ge(dve_step, C.last(dve_step))
                dve.reciprocal(s.z1[:], s.z1[:]).then_inc(C.give(dve_step), 1)
                dve.wait_ge(dve_step, C.last(dve_step))
                tt(s.work[:], probs, s.z1[:].unsqueeze(2).broadcast_to([128, SEQS, CTX]), ALU.mult)\
                    .then_inc(C.give(s.p_ready), 1)

            def normalise(s, src, dst, centre=True, to_pe=True):
                yield
                for b in range(SEQS):
                    dve.bn_stats(s.stats[:, b, :], src[:, b, :]).then_inc(C.give(dve_step), 1)
                dve.wait_ge(dve_step, C.last(dve_step))
                for b in range(SEQS):
                    ins = dve.bn_aggr(s.mv[:, b, :], s.stats[:, b, :])
                    if centre and b == SEQS - 1:
                        ins.then_inc(C.give(s.var_ready), 1)
                    else:
                        ins.then_inc(C.give(dve_step), 1)
                if not centre:
                    dve.wait_ge(dve_step, C.last(dve_step))
                    tt(s.msq[:], s.mv[:, :, 0], s.mv[:, :, 0], ALU.mult).then_inc(C.give(dve_step), 1)
                    dve.wait_ge(dve_step, C.last(dve_step))
                    tt(s.mv[:, :, 1], s.mv[:, :, 1], s.msq[:], ALU.add).then_inc(C.give(s.var_ready), 1)
                yield
                dve.wait_ge(s.rstd_ready, C.next(s.rstd_ready))
                for b in range(SEQS):
                    if centre:
                        ins = ts(dst[:, b, :], src[:, b, :], s.mv[:, b, 0:1], s.rstd[:, b:b + 1], ALU.subtract, ALU.mult)
                    else:
                        ins = ts(dst[:, b, :], src[:, b, :], s.rstd[:, b:b + 1], None, ALU.mult)
                    if b < SEQS - 1:
                        ins.then_inc(C.give(dve_step), 1)
                if to_pe:
                    ins.then_inc(C.give(s.n_ready), 1)
                else:
                    ins.then_inc(C.give(dve_step), 1)
                    dve.wait_ge(dve_step, C.last(dve_step))

            def take_subs(s, cols, scale, bias=None):
                dve.wait_ge(s.d_full, s.dve_d.take())
                o = s.dve_d.bank
                for j in range(SUBS):
                    src = o[:, 0:SEQS * cols].rearrange("p (b t) -> p b t", b=SEQS)
                    dst = s.sub_rows[:, :, j, 0:cols]
                    if bias is None:
                        ins = ts(dst, src, scale[:, j:j + 1], None, ALU.mult)
                    else:
                        ins = ts(dst, src, bias[:], scale[:, j:j + 1], ALU.add, ALU.mult)
                ins.then_inc(C.give(s.d_drained), 1)

            def per_head(v):
                return v.rearrange("p (g j d) -> p g j d", g=QUADS, j=SUBS)

            def unit_max(s, rows, width, b, j):
                dve.wait_ge(s.s_full, s.dve_s.take())
                o = s.dve_s.bank[0:rows, 0:4 * width].rearrange("p (g t) -> p g t", g=4)
                reduce(s.negmax[0:rows, b, 4 * j:4 * j + 4], o, ALU.max, negate=True).then_inc(C.give(s.max_ready), 1)

            def add_to_x(s):
                dve.wait_ge(s.d_full, s.dve_d.take())
                tt(s.xg[:], by_seq(s.dve_d.bank), s.xg[:], ALU.add).then_inc(C.give(s.d_drained), 1)
                dve.drain()

            def bias_to_x(s, bias):
                dve.drain()
                tt(s.xg[:], s.xg[:], bias[:].unsqueeze(1).broadcast_to([128, SEQS, CH]), ALU.add)\
                    .then_inc(C.give(dve_step), 1)
                dve.wait_ge(dve_step, C.last(dve_step))

            def causal_heads(s, keys, act_sums):
                n_units = SEQS * SUBS
                for u in range(n_units + (0 if act_sums else 2)):
                    if u < n_units:
                        yield
                        unit_max(s, TOK, keys, u // SUBS, u % SUBS)
                    if not act_sums and u >= 2:
                        yield
                        b, j = divmod(u - 2, SUBS)
                        dve.wait_ge(s.e_ready, C.next(s.e_ready))
                        reduce(s.zsum[:, b, 4 * j:4 * j + 4],
                               s.e[:, (u - 2) % 4, 0:4 * keys].rearrange("p (g t) -> p g t", g=4), ALU.add)\
                            .then_inc(C.give(dve_step), 1)
                if act_sums:
                    yield
                    dve.wait_ge(s.sums_ready, C.next(s.sums_ready))
                else:
                    dve.wait_ge(dve_step, C.last(dve_step))
                dve.reciprocal(s.rz[:], s.zsum[:]).then_inc(C.give(s.rz_ready), 1)
                yield
                dve.wait_ge(s.d_full, s.dve_d.take())
                o = s.dve_d.bank
                dve.wait_ge(s.rzB_ready, C.next(s.rzB_ready))
                tt(s.aT[:], o[:, 0:SEQS * TOK], s.rzB[:], ALU.mult).then_inc(C.give(s.d_drained), 1)

            def top2(s, mask, logits, rank, segs, n_):
                def view(t):
                    return t.rearrange("p (b s e) -> p b s e", b=SEQS, e=n_)

                size = SEQS * segs * n_
                first, t1, t2 = (view(s.tsel[:, i * size:(i + 1) * size]) for i in range(3))
                m = s.tm[:, 0, 0:SEQS * segs].rearrange("p (b s) -> p b s", b=SEQS)
                r = s.tm[:, 1, 0:SEQS * segs].rearrange("p (b s) -> p b s", b=SEQS)

                def wide(v):
                    return v.unsqueeze(3).broadcast_to([128, SEQS, segs, n_])
                src = logits
                for i in range(2):
                    yield
                    reduce(m, src, ALU.max).then_inc(C.give(dve_step), 1)
                    dve.wait_ge(dve_step, C.last(dve_step))
                    tt(t1, src, wide(m), ALU.is_ge).then_inc(C.give(dve_step), 1)
                    dve.wait_ge(dve_step, C.last(dve_step))
                    tt(t1, t1, rank, ALU.mult).then_inc(C.give(dve_step), 1)
                    dve.wait_ge(dve_step, C.last(dve_step))
                    reduce(r, t1, ALU.max).then_inc(C.give(dve_step), 1)
                    dve.wait_ge(dve_step, C.last(dve_step))
                    yield
                    tt(first if i == 0 else t1, t1, wide(r), ALU.is_equal).then_inc(C.give(dve_step), 1)
                    dve.wait_ge(dve_step, C.last(dve_step))
                    if i == 0:
                        ts(t2, first, -BIG, None, ALU.mult).then_inc(C.give(dve_step), 1)
                        dve.wait_ge(dve_step, C.last(dve_step))
                        tt(t2, t2, logits, ALU.add).then_inc(C.give(dve_step), 1)
                        dve.wait_ge(dve_step, C.last(dve_step))
                        src = t2
                tt(mask, first, t1, ALU.add).then_inc(C.give(dve_step), 1)
                dve.wait_ge(dve_step, C.last(dve_step))

            def quantise(dst, src, inverse, w):
                ts(w, src, inverse, ROUND, ALU.mult, ALU.add).then_inc(C.give(dve_step), 1)
                dve.wait_ge(dve_step, C.last(dve_step))
                ts(w, w, ROUND + QMAX, ROUND - QMAX - 1.0, ALU.min, ALU.max).then_inc(C.give(dve_step), 1)
                dve.wait_ge(dve_step, C.last(dve_step))
                return ts(dst, w, ROUND, None, ALU.subtract)

            def weights():
                scratch = q.e
                yield
                dve.wait_ge(loaded_q, NLOAD_Q)
                dve.drain()
                for w in range(2):
                    for t, (r0, m) in enumerate(ITILES):
                        yield
                        reduce(wscale[0:m, w, t:t + 1], wraw[0:m, w, t, :], ALU.max, apply_absolute_value=True).then_inc(C.give(dve_step), 1)
                        dve.wait_ge(dve_step, C.last(dve_step))
                        ts(wscale[0:m, w, t:t + 1], wscale[0:m, w, t:t + 1], 1.0 / QMAX, None, ALU.mult).then_inc(C.give(dve_step), 1)
                        dve.wait_ge(dve_step, C.last(dve_step))
                        dve.reciprocal(winv[0:m, w, t:t + 1], wscale[0:m, w, t:t + 1]).then_inc(C.give(dve_step), 1)
                        dve.wait_ge(dve_step, C.last(dve_step))
                        ins = quantise(wraw[0:m, w, t, :], wraw[0:m, w, t, :], winv[0:m, w, t:t + 1], scratch[0:m, 0, 0:128])
                        if t < 2:
                            ins.then_inc(C.give(dve_step), 1)
                            dve.wait_ge(dve_step, C.last(dve_step))
                    ins.then_inc(C.give(w_ready), 1)
                    dve.drain()
                yield
                reduce(dscale[:], wdraw[:], ALU.max, apply_absolute_value=True).then_inc(C.give(dve_step), 1)
                dve.wait_ge(dve_step, C.last(dve_step))
                ts(dscale[:], dscale[:], 1.0 / QMAX, None, ALU.mult).then_inc(C.give(dve_step), 1)
                dve.wait_ge(dve_step, C.last(dve_step))
                dve.reciprocal(winv[:, 0, 0:1], dscale[:]).then_inc(C.give(dve_step), 1)
                dve.wait_ge(dve_step, C.last(dve_step))
                quantise(wdraw[:], wdraw[:], winv[:, 0, 0:1], scratch[:, 0, 0:INNER]).then_inc(C.give(w_ready), 1)
                yield
                dve.memset(dscaleB[:], 1.0).then_inc(C.give(dve_step), 1)
                dve.wait_ge(dve_step, C.last(dve_step))
                ts(dscaleB[:], dscaleB[:], dscale[:], None, ALU.mult).then_inc(C.give(w_ready), 1)
            def hand_over():
                dve.tensor_copy(q.xg[:], p.xg[:])
                dve.tensor_copy(q.ctxT[:], p.ctxT[:])
                dve.tensor_copy(q.ctxg[:], p.ctxg[:])
                dve.drain().then_inc(C.give(handed), 1)

            def layers_p(s):
                yield
                dve.wait_ge(s.x_in, 16)
                dve.sem_inc(s.x_in, -16)
                yield from normalise(s, s.xg, s.n)
                yield
                bias_to_x(s, b0o)
                take_subs(s, CTX, subscale, b0k)
                yield
                dve.wait_ge(s.d_full, s.dve_d.take())
                tt(s.vg[0:CTX], by_seq(s.dve_d.bank)[0:CTX],
                   b0v[0:CTX].unsqueeze(1).broadcast_to([CTX, SEQS, CH]), ALU.add).then_inc(C.give(s.d_drained), 1)
                dve.drain()
                for place, kind, u in L0X_STEPS_DVE:
                    yield
                    b, j = divmod(u, SUBS)
                    if kind == "scores":
                        unit_max(s, CTX, TOK, b, j)
                    else:
                        dve.wait_ge(s.sums_ready, C.next(s.sums_ready))
                        dve.reciprocal(s.rz[0:CTX, b, :], s.zsum[0:CTX, b, :]).then_inc(C.give(dve_step), 1)
                        dve.wait_ge(dve_step, C.last(dve_step))
                        tt(s.vdiag[0:CTX, b].rearrange("p g (j c) -> p g j c", j=SUBS)[:, :, :, 0:HDIM],
                           per_head(s.vg[0:CTX, b, :]),
                           s.rz[0:CTX, b, :].rearrange("p (j g) -> p g j", j=SUBS).unsqueeze(3)
                           .broadcast_to([CTX, QUADS, SUBS, HDIM]), ALU.mult).then_inc(C.give(s.v_ready), 1)
                yield
                add_to_x(s)

                yield from normalise(s, s.xg, s.n)
                yield
                dve.wait_ge(s.xv_ready, C.next(s.xv_ready))
                dve.drain()
                yield from top2(s, s.gates[:], s.xvs[:, :, NV:].rearrange("p b (s e) -> p b s e", e=SE),
                                rank5[:].rearrange("p (b s) e -> p b s e", b=SEQS), 2 * SH, SE)
                yield
                dve.wait_ge(s.sig_ready, C.next(s.sig_ready))
                ts(s.gexp[:], s.gexp[:], 1.0, None, ALU.add).then_inc(C.give(dve_step), 1)
                dve.wait_ge(dve_step, C.last(dve_step))
                dve.reciprocal(s.gexp[:], s.gexp[:]).then_inc(C.give(dve_step), 1)
                dve.wait_ge(dve_step, C.last(dve_step))
                tt(s.gates[:, :, 0:SH, :], s.gates[:, :, 0:SH, :], s.gexp[:], ALU.mult).then_inc(C.give(s.gate_ready), 1)
                for t in range(4):
                    yield
                    dve.wait_ge(s.s_full, s.dve_s.take())
                    dve.tensor_copy(s.kf[:, t, :], s.dve_s.bank[:, 0:SEQS * TOK]).then_inc(C.give(s.s_drained), 1)
                n_units = 2 * SEQS
                for u in range(n_units + 2):
                    yield
                    if u < n_units:
                        unit_max(s, TOK, TOK, u // 2, u % 2)
                    v = u - 2
                    if 0 <= v < n_units and v % 2 == 1:
                        yield
                        b = v // 2
                        dve.wait_ge(s.sums_ready, C.next(s.sums_ready))
                        dve.reciprocal(s.rz[:, b, 0:SH], s.zsum[:, b, 0:SH]).then_inc(C.give(dve_step), 1)
                        dve.wait_ge(dve_step, C.last(dve_step))
                        og = s.gates[:, b, SH:, :].rearrange("p (t q) e -> p t q e", q=2)
                        tt(og, og, s.rz[:, b, 0:SH].rearrange("p (q t) -> p t q", q=2).unsqueeze(3)
                           .broadcast_to([128, 4, 2, SE]), ALU.mult).then_inc(C.give(s.ogate_ready), 1)
                    if u % 2 == 0 and u >= 4:
                        yield
                        gated_sum(s, u // 2 - 2)
                yield
                gated_sum(s, SEQS - 1)
                yield
                dve.drain().then_inc(C.give(s.y_ready), 1)
                yield
                add_to_x(s)

            def layers_q(s, it):
                yield
                dve.wait_ge(s.n_read, C.next(s.n_read))
                dve.drain()
                yield from normalise(s, s.xg, s.n)
                yield
                bias_to_x(s, b1o)
                dve.wait_ge(s.d_full, s.dve_d.take())
                dve.tensor_copy(s.vg[0:CTX], by_seq(s.dve_d.bank)[0:CTX]).then_inc(C.give(s.d_drained), 1)
                yield
                dve.wait_ge(s.d_full, s.dve_d.take())
                ts(s.sc[:], s.dve_d.bank[:, 0:SEQS * CTX].rearrange("p (b s) -> p b s", b=SEQS),
                   float(CH) ** -0.5, None, ALU.mult).then_inc(C.give(s.d_drained), 1)
                dve.drain()
                for r in range(TOPK // 8):
                    yield
                    src = s.sc if r == 0 else s.work
                    for b in range(SEQS):
                        dve.max(s.top8[:, b, r, :], src[:, b, :]).then_inc(C.give(dve_step), 1)
                    dve.wait_ge(dve_step, C.last(dve_step))
                    if r == 0:
                        ts(s.negmax[:, :, 0], s.top8[:, :, 0, 0], -1.0, None, ALU.mult).then_inc(C.give(s.pmax_ready), 1)
                    for b in range(SEQS):
                        dve.match_replace(s.work[:, b, :], s.top8[:, b, r, :], src[:, b, :], -BIG).then_inc(C.give(dve_step), 1)
                    dve.wait_ge(dve_step, C.last(dve_step))
                yield
                dve.wait_ge(s.pexp_ready, C.next(s.pexp_ready))
                for b in range(SEQS):
                    stt(out=s.work[:, b, :], in0=s.work[:, b, :], scalar=-BIG, in1=s.e[:, 0, b * CTX:(b + 1) * CTX],
                        op0=ALU.is_equal, op1=ALU.mult).then_inc(C.give(dve_step), 1)
                dve.wait_ge(dve_step, C.last(dve_step))
                softmax_scale(s, s.work[:])
                yield
                add_to_x(s)

                yield
                dve.wait_ge(s.x_stored, 16)
                dve.sem_inc(s.x_stored, -16)
                yield from normalise(s, s.xg, s.hres, to_pe=False)
                yield from normalise(s, s.hres, s.n, centre=False)
                yield
                take_subs(s, TOK, subscale)
                yield
                dve.wait_ge(s.d_full, s.dve_d.take())
                o = s.dve_d.bank
                for j in range(SUBS):
                    ins = dve.tensor_copy(s.vdiag[:, :, :, 40 * j:40 * j + HDIM],
                                          o[:, 0:SEQS * 32].rearrange("p (b g d) -> p b g d", b=SEQS, g=QUADS))
                ins.then_inc(C.give(s.d_drained), 1)
                yield from causal_heads(s, TOK, act_sums=True)
                yield
                dve.wait_ge(s.d_full, s.dve_d.take())
                tt(s.hres[:], by_seq(s.dve_d.bank), s.hres[:], ALU.add).then_inc(C.give(s.d_drained), 1)
                dve.drain()
                yield from normalise(s, s.hres, s.n, centre=False)
                tt(s.xg[:], s.xg[:], s.hres[:], ALU.add).then_inc(C.give(dve_step), 1)
                yield
                dve.wait_ge(s.d_full, s.dve_d.take())
                dve.tensor_copy(s.clog[:], s.dve_d.bank[:, 0:SEQS * ME].rearrange("p (b e) -> p b e", b=SEQS)).then_inc(C.give(s.d_drained), 1)
                dve.drain()
                reduce(s.z1[:], s.clog[:], ALU.max).then_inc(C.give(dve_step), 1)
                yield from top2(s, s.comb[:].unsqueeze(2), s.clog[:].unsqueeze(2), rank8[:].unsqueeze(2), 1, ME)
                tt(s.clog[:], s.clog[:], s.z1[:].unsqueeze(2).broadcast_to([128, SEQS, ME]),
                   ALU.subtract).then_inc(C.give(s.c_ready), 1)
                yield
                dve.wait_ge(s.cexp_ready, C.next(s.cexp_ready))
                tt(s.comb[:], s.comb[:], s.clog[:], ALU.mult).then_inc(C.give(dve_step), 1)
                dve.wait_ge(dve_step, C.last(dve_step))
                reduce(s.z1[:], s.comb[:], ALU.add).then_inc(C.give(dve_step), 1)
                dve.wait_ge(dve_step, C.last(dve_step))
                dve.reciprocal(s.z1[:], s.z1[:]).then_inc(C.give(dve_step), 1)
                dve.wait_ge(dve_step, C.last(dve_step))
                tt(s.comb[:], s.comb[:], s.z1[:].unsqueeze(2).broadcast_to([128, SEQS, ME]), ALU.mult).then_inc(C.give(dve_step), 1)
                dve.wait_ge(dve_step, C.last(dve_step))
                for i in range(2 * SEQS):
                    b, half = divmod(i, 2)
                    yield
                    dve.wait_ge(s.s_full, s.dve_s.take())
                    o = s.dve_s.bank
                    for ex in range(4):
                        w = 4 * half + ex
                        ins = stt(out=s.xg[:, b, :], in0=o[:, ex * 128:(ex + 1) * 128], scalar=s.comb[:, b, w:w + 1],
                                  in1=s.xg[:, b, :], op0=ALU.mult, op1=ALU.add)
                        if ex < 3:
                            ins.then_inc(C.give(dve_step), 1)
                            dve.wait_ge(dve_step, C.last(dve_step))
                    ins.then_inc(C.give(s.s_drained), 1)
                    dve.drain()

                yield from normalise(s, s.xg, s.n)
                yield
                dve.wait_ge(s.d_full, s.dve_d.take())
                dve.tensor_copy(s.sc[:], s.dve_d.bank[:, 0:SEQS * CTX].rearrange("p (b s) -> p b s", b=SEQS)).then_inc(C.give(s.d_drained), 1)
                dve.drain()
                reduce(s.negmax[:, :, 0], s.sc[:], ALU.max, negate=True).then_inc(C.give(s.pmax_ready), 1)
                yield
                dve.wait_ge(s.pexp_ready, C.next(s.pexp_ready))
                softmax_scale(s, s.e[:, 0, 0:SEQS * CTX].rearrange("p (b s) -> p b s", b=SEQS))
                yield
                dve.wait_ge(s.d_full, s.dve_d.take())
                tt(s.hres[:], by_seq(s.dve_d.bank), s.xg[:], ALU.add).then_inc(C.give(s.d_drained), 1)
                dve.drain().then_inc(C.give(x_ready), 1)
                yield from normalise(s, s.hres, s.n)
                dve.drain()
                reduce(amax[:, bass.ds(it, 1)], s.n[:].rearrange("p b c -> p (b c)"), ALU.max,
                       apply_absolute_value=True)

            def gated_sum(s, b):
                dve.wait_ge(s.av_dve, C.next(s.av_dve))
                dve.drain()
                for ex in range(POOL_OUT, SE):
                    tt(oprod[:, ex, :].rearrange("p (h k) -> p h k", h=SH),
                       s.av[:, b % 2, :].rearrange("p (h k) -> p h k", h=SH),
                       s.gates[:, b, SH:, ex].unsqueeze(2).broadcast_to([128, SH, SHD]), ALU.mult)\
                        .then_inc(C.give(dve_step), 1)
                dve.wait_ge(oprod_ready, C.next(oprod_ready))
                dve.wait_ge(dve_step, C.last(dve_step))
                reduce(s.ys[:, b, :].rearrange("p (e k) -> p e k", e=SE),
                       oprod[:].rearrange("p e (h k) -> p e k h", h=SH), ALU.add).then_inc(C.give(oprod_free), 1)

            def settle_p():
                settle(p, p.rstd_ready, p.sums_ready, p.xv_ready, p.sig_ready, p.av_dve, oprod_ready)

            def settle_q():
                settle(q, q.n_read, q.rstd_ready, q.sums_ready, q.pexp_ready, q.rzB_ready, q.cexp_ready)

            C.section = "A, first"
            in_order(ORDER["first", "vector"], layers_p(p), weights())
            settle_p()
            settle_steps()
            C.section = "A"
            with dve.Fori(1, NGROUPS) as it:
                dve.drain()
                hand_over()
                dve.drain().then_inc(C.give(p_free), 1)
                in_order(ORDER["A", "vector"], layers_p(p), layers_q(q, it - 1))
                settle_p()
                settle_q()
                settle_steps()
            C.section = "A, last"
            dve.drain()
            hand_over()
            alone(layers_q(q, NGROUPS - 1))
            settle_q()
            settle_steps()
            dve.wait_ge(q.x_stored, 16)
            dve.sem_inc(q.x_stored, -16)
            dve.drain().then_inc(x_safe, 1)

            def act_scale(i):
                a = actscale[:, 6 + i:7 + i]
                tt(a, gmax[:, 2 * i + 1:2 * i + 2], sigm[:, i:i + 1], ALU.mult).then_inc(C.give(dve_step), 1)
                dve.wait_ge(dve_step, C.last(dve_step))
                ts(a, a, 1.0 / QMAX, None, ALU.mult).then_inc(C.give(dve_step), 1)
                dve.wait_ge(dve_step, C.last(dve_step))
                dve.reciprocal(ainv[:, i:i + 1], a).then_inc(C.give(dve_step), 1)
                dve.wait_ge(dve_step, C.last(dve_step))

            C.section = "AB"
            dve.drain()
            reduce(gmax[:, 0:1], amax[:], ALU.max).then_inc(amax_ready, 1)
            dve.wait_ge(clip_exp, 1)
            ts(sigm[:], clipe[:], 1.0, None, ALU.add).then_inc(C.give(dve_step), 1)
            dve.wait_ge(dve_step, C.last(dve_step))
            dve.reciprocal(sigm[:], sigm[:]).then_inc(C.give(dve_step), 1)
            dve.wait_ge(dve_step, C.last(dve_step))
            dve.wait_ge(gmax_ready, 1)
            act_scale(0)
            for t, (r0, m) in enumerate(ITILES):
                ts(upscale[0:m, t:t + 1], wscale[0:m, 1, t:t + 1], actscale[0:m, 6:7], None, ALU.mult).then_inc(C.give(dve_step), 1)
                ins = ts(actscale[0:m, t:t + 1], wscale[0:m, 0, t:t + 1], actscale[0:m, 6:7], None, ALU.mult)
            ins.then_inc(sx_ready, 1)
            settle_steps()

            def layers_b(s, it):
                group = it * 2 + s.index
                cols = bass.ds(group * SEQS * TOK, SEQS * TOK)
                yield
                quantise(s.xq[:], nT_all[:, cols], ainv[:, 0:1], s.e[:, 0, :]).then_inc(C.give(s.q_ready), 1)
                for t, (r0, m) in enumerate(ITILES):
                    yield
                    h = s.e[0:m, 1 + t % 2, :]
                    dve.wait_ge(s.d_full, s.dve_d.take())
                    o = s.dve_d.bank
                    dve.wait_ge(s.sil_ready, C.next(s.sil_ready))
                    stt(out=h, in0=o[0:m, :], scalar=upscale[0:m, t:t + 1], in1=s.eT[0:m, t % 2, :],
                        op0=ALU.mult, op1=ALU.mult).then_inc(C.give(s.d_drained), 1)
                    dve.drain()
                    dve.tensor_copy(h_all[0:m, t, cols], h).then_inc(C.give(dve_step), 1)
                    reduce(hmax[0:m, bass.ds(group * 3 + t, 1)], h, ALU.max, apply_absolute_value=True)\
                        .then_inc(C.give(dve_step), 1)
                    dve.wait_ge(dve_step, C.last(dve_step))

            C.section = "B"
            with dve.Fori(0, NGROUPS // 2) as it:
                dve.drain()
                in_order(ORDER["B", "vector"], layers_b(p, it), layers_b(q, it))
                for s in streams:
                    settle(s, s.sil_ready)
                settle_steps()

            C.section = "BC"
            dve.drain()
            reduce(gmax[:, 2:3], hmax[:], ALU.max).then_inc(amax_ready, 1)
            dve.wait_ge(gmax_ready, 2)
            act_scale(1)
            ts(dscaleB[:], dscaleB[:], actscale[:, 7:8], None, ALU.mult).then_inc(C.give(dve_step), 1)
            settle_steps()

            def layers_c(s, it):
                group = it * 2 + s.index
                yield
                for t, (r0, m) in enumerate(ITILES):
                    ins = quantise(s.hq[0:m, t, :], h_all[0:m, t, bass.ds(group * SEQS * TOK, SEQS * TOK)],
                                   ainv[0:m, 1:2], s.wk32[0:m, t, :])
                    if t < 2:
                        ins.then_inc(C.give(dve_step), 1)
                ins.then_inc(C.give(s.q_ready), 1)
                yield
                dve.wait_ge(s.x_stored, 16)
                dve.sem_inc(s.x_stored, -16)
                dve.wait_ge(s.d_full, s.dve_d.take())
                tt(s.n[:], by_seq(s.dve_d.bank),
                   dscaleB[:].unsqueeze(1).broadcast_to([128, SEQS, CH]), ALU.mult).then_inc(C.give(s.d_drained), 1)
                dve.wait_ge(s.x_in, 16)
                dve.sem_inc(s.x_in, -16)
                dve.drain()
                tt(s.xg[:], s.xg[:], s.n[:], ALU.add).then_inc(C.give(dve_step), 1)
                dve.wait_ge(dve_step, C.last(dve_step))
                yield from normalise(s, s.xg, s.n)
                yield
                dve.wait_ge(s.d_full, s.dve_d.take())
                o = s.dve_d.bank
                for j in range(SUBS):
                    ins = dve.tensor_copy(s.vdiag[0:CTX, :, :, 40 * j:40 * j + HDIM],
                                          o[0:CTX, 0:SEQS * CH].rearrange("p (b g j d) -> p b g j d", b=SEQS, g=QUADS,
                                                                          j=SUBS)[:, :, :, j, :])
                ins.then_inc(C.give(s.d_drained), 1)
                yield
                take_subs(s, TOK, subscale)
                yield from causal_heads(s, CTX, act_sums=False)
                yield
                add_to_x(s)
                yield from normalise(s, s.xg, s.n)
                bias_to_x(s, b32)
                for t in (1, 3):
                    yield
                    dve.wait_ge(s.d_full, s.dve_d.take())
                    ts(s.hid[:, t, :], s.dve_d.bank[:], b31[:, t:t + 1], 0.0, ALU.add, ALU.max)                        .then_inc(C.give(s.d_drained), 1)
                yield
                dve.wait_ge(s.d_full, s.dve_d.take())
                tt(s.n[:], by_seq(s.dve_d.bank), s.xg[:], ALU.add).then_inc(C.give(s.d_drained), 1)
                dve.drain().then_inc(C.give(s.x_done), 1)

            C.section = "C"
            for s in streams:
                dve.sem_inc(s.x_stored, 16)
            with dve.Fori(0, NGROUPS // 2) as it:
                in_order(ORDER["C", "vector"], layers_c(p, it), layers_c(q, it))
                for s in streams:
                    settle(s, s.rstd_ready, s.e_ready, s.rzB_ready)
                settle_steps()
            dve.wait_ge(p.x_stored, 16)
            dve.wait_ge(q.x_stored, 16)

        C.check()
    return nc


def kernel(**inputs):
    import numpy as np
    import concourse.bacc as bacc
    from concourse.bass_utils import run_bass_kernel_spmd

    nc = bacc.Bacc("TRN2", target_bir_lowering=False, num_devices=1)
    turned = {"L1_xattn_Wq", "L1_xattn_Wk", "L1_xattn_Wv", "L1_xattn_Wo", "L1_ffn_wq", "L1_ffn_wk", "L1_ffn_wv",
              "L1_ffn_wo", "L1_ffn_gate_w", "L3_xattn_Wq", "L3_xattn_Wk", "L3_xattn_Wv", "L3_xattn_Wo"}
    arrays, d = {}, {}
    for name, value in inputs.items():
        a = np.asarray(value)
        if name in turned:
            a = a.T
        if name == "L1_ffn_expert_w":
            a = a.transpose(0, 2, 1)
        a = np.ascontiguousarray(a)
        arrays["in_" + name] = a
        d[name] = nc.dram_tensor("in_" + name, a.shape, mybir.dt.from_np(a.dtype), kind="ExternalInput").ap()
    out = nc.dram_tensor("out", (BATCH, TOK, CH), FP32, kind="ExternalOutput").ap()
    four_layers(nc, d, out)
    r = run_bass_kernel_spmd(nc, [arrays], core_ids=[0])
    return r.results[0]["out"]
```
